# Optimizing a Trainium2 kernel written in Bass

```python
import numpy as np
import jax
import jax.numpy as jnp

def _softmax(x, axis=-1):
    return jax.nn.softmax(x, axis=axis)

def _gelu(x):
    return jax.nn.gelu(x, approximate=True)

def _silu(x):
    return jax.nn.silu(x)

def _sigmoid(x):
    return jax.nn.sigmoid(x)

def _layernorm(x, axis=-1, eps=1e-05):
    m = jnp.mean(x, axis=axis, keepdims=True)
    v = jnp.var(x, axis=axis, keepdims=True)
    return (x - m) / jnp.sqrt(v + eps)

def _scatter_add(tgt, idx, src, axis=0):
    return tgt.at[idx].add(src)

def _segment_sum(src, seg, n):
    return jax.ops.segment_sum(src, seg, n)
kernel_name = 'mk_adaln_d2_jaxref_r8_f45a03'

def setup_inputs(seed: int=0):
    np.random.seed(seed)
    _w = jnp.asarray

    def _L0_attn_setup():
        import jax, jax.numpy as jnp
        import numpy as np
        BH = 32
        BW = 32
        key = jax.random.key(seed)
        k1, k2, k3, k4 = jax.random.split(key, 4)
        B, S, K, N = (2, 256, 512, 512)
        data = jax.random.normal(k1, (B, S, K), dtype=jnp.float32)
        weight = jax.random.normal(k2, (N, K), dtype=jnp.float32) * 0.02
        bias = jax.random.normal(k3, (N,), dtype=jnp.float32) * 0.02
        Nb, Kb = (N // BH, K // BW)
        block_on = jax.random.uniform(k4, (Nb, Kb)) < 0.3
        mask = jnp.repeat(jnp.repeat(block_on, BH, axis=0), BW, axis=1).astype(jnp.int32)
        return {'data': data, 'mask': mask, 'weight': weight, 'bias': bias}
    _L0_attn_in = _L0_attn_setup()

    def _L0_ffn_setup():
        import jax, jax.numpy as jnp
        import numpy as np
        D_MODEL = 512
        D_HIDDEN = 1376
        RANK = 16
        BATCH, SEQ = (2, 256)

        def _matmul_lora(x, w, a, b, scale=1.0):
            out = jnp.einsum('bsd,hd->bsh', x, w)
            out = out + jnp.einsum('bsr,hr->bsh', jnp.einsum('bsd,rd->bsr', x, a), b) * scale
            return out
        key = jax.random.key(seed)
        ks = jax.random.split(key, 10)
        s = 0.02
        return {'x': jax.random.normal(ks[0], (BATCH, SEQ, D_MODEL), jnp.float32), 'gate_w': jax.random.normal(ks[1], (D_HIDDEN, D_MODEL), jnp.float32) * s, 'up_w': jax.random.normal(ks[2], (D_HIDDEN, D_MODEL), jnp.float32) * s, 'down_w': jax.random.normal(ks[3], (D_MODEL, D_HIDDEN), jnp.float32) * s, 'gate_a': jax.random.normal(ks[4], (RANK, D_MODEL), jnp.float32) * s, 'gate_b': jax.random.normal(ks[5], (D_HIDDEN, RANK), jnp.float32) * s, 'up_a': jax.random.normal(ks[6], (RANK, D_MODEL), jnp.float32) * s, 'up_b': jax.random.normal(ks[7], (D_HIDDEN, RANK), jnp.float32) * s, 'down_a': jax.random.normal(ks[8], (RANK, D_HIDDEN), jnp.float32) * s, 'down_b': jax.random.normal(ks[9], (D_MODEL, RANK), jnp.float32) * s}
    _L0_ffn_in = _L0_ffn_setup()
    _L0_c = _w((lambda *s: np.random.randn(*s).astype(np.float32) * 0.05)(1, 512))
    _L0_wmod = _w((lambda *s: np.random.randn(*s).astype(np.float32) * 0.05)(512, 6 * 512) * 512 ** (-0.5))

    def _L1_attn_setup():
        import jax, jax.numpy as jnp
        import numpy as np
        H = 512
        D_IN = 1024
        N = 16
        K = 4
        R = 32
        EPS = 1e-06

        def rms_forward(x, eps=EPS):
            xf = x.astype(jnp.float32)
            var = jnp.mean(xf * xf, axis=-1, keepdims=True)
            return (xf * jax.lax.rsqrt(var + eps)).astype(x.dtype)
        key = jax.random.key(seed)
        ks = jax.random.split(key, 10)
        s = 0.02
        hidden_states = jax.random.normal(ks[0], (2, 128, H), dtype=jnp.float32)
        W_in = jax.random.normal(ks[1], (2 * D_IN, H), dtype=jnp.float32) * s
        conv_w = jax.random.normal(ks[2], (D_IN, K), dtype=jnp.float32) * 0.2
        conv_b = jax.random.normal(ks[3], (D_IN,), dtype=jnp.float32) * 0.02
        W_x = jax.random.normal(ks[4], (R + 2 * N, D_IN), dtype=jnp.float32) * s
        W_dt = jax.random.normal(ks[5], (D_IN, R), dtype=jnp.float32) * s
        b_dt = jax.random.normal(ks[6], (D_IN,), dtype=jnp.float32) * 0.02
        A_log = jnp.log(jnp.broadcast_to(jnp.arange(1, N + 1, dtype=jnp.float32)[None, :], (D_IN, N)))
        D = jnp.ones((D_IN,), dtype=jnp.float32)
        W_out = jax.random.normal(ks[7], (H, D_IN), dtype=jnp.float32) * s
        return {'hidden_states': hidden_states, 'W_in': W_in, 'conv_w': conv_w, 'conv_b': conv_b, 'W_x': W_x, 'W_dt': W_dt, 'b_dt': b_dt, 'A_log': A_log, 'D': D, 'W_out': W_out}
    _L1_attn_in = _L1_attn_setup()

    def _L1_ffn_setup():
        import jax, jax.numpy as jnp
        import numpy as np
        R = 16
        ALPHA = 32
        SCALING = ALPHA / R
        E = 8
        TOP_K = 2
        key = jax.random.key(seed)
        ks = jax.random.split(key, 5)
        B, S, D = (4, 256, 512)
        x = jax.random.normal(ks[0], (B, S, D), dtype=jnp.float32)
        base_W = jax.random.normal(ks[1], (D, D), dtype=jnp.float32) * 0.02
        router_W = jax.random.normal(ks[2], (E, D), dtype=jnp.float32) * 0.02
        lora_A = jax.random.normal(ks[3], (E, D, R), dtype=jnp.float32) * 0.02
        lora_B = jax.random.normal(ks[4], (E, R, D), dtype=jnp.float32) * 0.02
        return {'x': x, 'base_W': base_W, 'router_W': router_W, 'lora_A': lora_A, 'lora_B': lora_B}
    _L1_ffn_in = _L1_ffn_setup()
    _L1_c = _w((lambda *s: np.random.randn(*s).astype(np.float32) * 0.05)(1, 512))
    _L1_wmod = _w((lambda *s: np.random.randn(*s).astype(np.float32) * 0.05)(512, 6 * 512) * 512 ** (-0.5))
    _d = {'L0_attn_data': _L0_attn_in['data'], 'L0_attn_mask': _L0_attn_in['mask'], 'L0_attn_weight': _L0_attn_in['weight'], 'L0_attn_bias': _L0_attn_in['bias'], 'L0_ffn_gate_w': _L0_ffn_in['gate_w'], 'L0_ffn_up_w': _L0_ffn_in['up_w'], 'L0_ffn_down_w': _L0_ffn_in['down_w'], 'L0_ffn_gate_a': _L0_ffn_in['gate_a'], 'L0_ffn_gate_b': _L0_ffn_in['gate_b'], 'L0_ffn_up_a': _L0_ffn_in['up_a'], 'L0_ffn_up_b': _L0_ffn_in['up_b'], 'L0_ffn_down_a': _L0_ffn_in['down_a'], 'L0_ffn_down_b': _L0_ffn_in['down_b'], 'L0_c': _L0_c, 'L0_wmod': _L0_wmod, 'L1_attn_W_in': _L1_attn_in['W_in'], 'L1_attn_conv_w': _L1_attn_in['conv_w'], 'L1_attn_conv_b': _L1_attn_in['conv_b'], 'L1_attn_W_x': _L1_attn_in['W_x'], 'L1_attn_W_dt': _L1_attn_in['W_dt'], 'L1_attn_b_dt': _L1_attn_in['b_dt'], 'L1_attn_A_log': _L1_attn_in['A_log'], 'L1_attn_D': _L1_attn_in['D'], 'L1_attn_W_out': _L1_attn_in['W_out'], 'L1_ffn_base_W': _L1_ffn_in['base_W'], 'L1_ffn_router_W': _L1_ffn_in['router_W'], 'L1_ffn_lora_A': _L1_ffn_in['lora_A'], 'L1_ffn_lora_B': _L1_ffn_in['lora_B'], 'L1_c': _L1_c, 'L1_wmod': _L1_wmod}
    _x0 = _d['L0_attn_data']
    _d['L0_attn_data'] = jax.random.normal(jax.random.fold_in(jax.random.key(seed), 1), (1, 2048, 512), dtype=_x0.dtype)
    del _x0
    return _d

def reference(L0_attn_data, L0_attn_mask, L0_attn_weight, L0_attn_bias, L0_ffn_gate_w, L0_ffn_up_w, L0_ffn_down_w, L0_ffn_gate_a, L0_ffn_gate_b, L0_ffn_up_a, L0_ffn_up_b, L0_ffn_down_a, L0_ffn_down_b, L0_c, L0_wmod, L1_attn_W_in, L1_attn_conv_w, L1_attn_conv_b, L1_attn_W_x, L1_attn_W_dt, L1_attn_b_dt, L1_attn_A_log, L1_attn_D, L1_attn_W_out, L1_ffn_base_W, L1_ffn_router_W, L1_ffn_lora_A, L1_ffn_lora_B, L1_c, L1_wmod):

    def _L0_attn_ref(data, mask, weight, bias):
        import jax, jax.numpy as jnp
        import numpy as np
        BH = 32
        BW = 32
        N, K = weight.shape
        Nb, Kb = (N // BH, K // BW)
        bm = mask.reshape(Nb, BH, Kb, BW).sum(axis=(1, 3)) > 0
        wb = weight.reshape(Nb, BH, Kb, BW) * bm[:, None, :, None].astype(weight.dtype)
        w = wb.reshape(N, K)
        out = jnp.einsum('bsk,nk->bsn', data, w) + bias
        return out

    def _L0_ffn_ref(x, gate_w, up_w, down_w, gate_a, gate_b, up_a, up_b, down_a, down_b):
        import jax, jax.numpy as jnp
        import numpy as np
        D_MODEL = 512
        D_HIDDEN = 1376
        RANK = 16
        BATCH, SEQ = (2, 256)

        def _matmul_lora(x, w, a, b, scale=1.0):
            out = jnp.einsum('bsd,hd->bsh', x, w)
            out = out + jnp.einsum('bsr,hr->bsh', jnp.einsum('bsd,rd->bsr', x, a), b) * scale
            return out
        gate = _matmul_lora(x, gate_w, gate_a, gate_b)
        up = _matmul_lora(x, up_w, up_a, up_b)
        hidden = jax.nn.silu(gate) * up
        out = _matmul_lora(hidden, down_w, down_a, down_b)
        return out

    def _L1_attn_ref(hidden_states, W_in, conv_w, conv_b, W_x, W_dt, b_dt, A_log, D, W_out):
        import jax, jax.numpy as jnp
        import numpy as np
        H = 512
        D_IN = 1024
        N = 16
        K = 4
        R = 32
        EPS = 1e-06

        def rms_forward(x, eps=EPS):
            xf = x.astype(jnp.float32)
            var = jnp.mean(xf * xf, axis=-1, keepdims=True)
            return (xf * jax.lax.rsqrt(var + eps)).astype(x.dtype)
        b, L, _ = hidden_states.shape
        proj = hidden_states @ W_in.T
        x, gate = (proj[..., :D_IN], proj[..., D_IN:])
        xpad = jnp.pad(x, ((0, 0), (K - 1, 0), (0, 0)))
        xc = conv_b
        for j in range(K):
            xc = xc + conv_w[:, j] * xpad[:, j:j + L, :]
        x = jax.nn.silu(xc)
        ssm = x @ W_x.T
        ts, Bm, Cm = (ssm[..., :R], ssm[..., R:R + N], ssm[..., R + N:])
        ts = rms_forward(ts)
        Bm = rms_forward(Bm)
        Cm = rms_forward(Cm)
        dt = jax.nn.softplus(ts @ W_dt.T + b_dt)
        A = -jnp.exp(A_log.astype(jnp.float32))

        def step(state, inp):
            dt_t, B_t, C_t, u_t = inp
            dA = jnp.exp(dt_t[..., None] * A)
            state = state * dA + (dt_t * u_t)[..., None] * B_t[:, None, :]
            y = jnp.einsum('bdn,bn->bd', state, C_t)
            return (state, y)
        init = jnp.zeros((b, D_IN, N), dtype=jnp.float32)
        xs = (dt.transpose(1, 0, 2), Bm.transpose(1, 0, 2), Cm.transpose(1, 0, 2), x.transpose(1, 0, 2))
        _, ys = jax.lax.scan(step, init, xs)
        y = ys.transpose(1, 0, 2) + x * D
        y = y * jax.nn.silu(gate)
        return y @ W_out.T

    def _L1_ffn_ref(x, base_W, router_W, lora_A, lora_B):
        import jax, jax.numpy as jnp
        import numpy as np
        R = 16
        ALPHA = 32
        SCALING = ALPHA / R
        E = 8
        TOP_K = 2
        base = jnp.einsum('bsd,od->bso', x, base_W)
        logits = jnp.einsum('bsd,ed->bse', x, router_W)
        probs = jax.nn.softmax(logits.astype(jnp.float32), axis=-1)
        top_vals, top_idx = jax.lax.top_k(probs, TOP_K)
        rw = top_vals / jnp.sum(top_vals, axis=-1, keepdims=True)
        w_dense = jnp.sum(jax.nn.one_hot(top_idx, E, dtype=rw.dtype) * rw[..., None], axis=-2).astype(x.dtype)
        mid = jnp.einsum('bsd,edr->bser', x, lora_A)
        mid = mid * w_dense[..., None]
        inc = jnp.einsum('bser,erd->bsd', mid, lora_B)
        return base + inc * SCALING
    x = L0_attn_data
    mod = (_silu(L0_c) @ L0_wmod).reshape(L0_c.shape[0], 6, 1, -1)
    sa, ca, ga, sb, cb, gb = (mod[:, 0], mod[:, 1], mod[:, 2], mod[:, 3], mod[:, 4], mod[:, 5])
    ga = (2 * (ga >= 0) - 1) * jnp.maximum(jnp.abs(ga), 0.25)
    gb = (2 * (gb >= 0) - 1) * jnp.maximum(jnp.abs(gb), 0.25)
    h = _layernorm(x, axis=-1) * (1 + ca) + sa
    x = x + ga * _L0_attn_ref(h, L0_attn_mask, L0_attn_weight, L0_attn_bias)
    h = _layernorm(x, axis=-1) * (1 + cb) + sb
    x = x + gb * _L0_ffn_ref(h, L0_ffn_gate_w, L0_ffn_up_w, L0_ffn_down_w, L0_ffn_gate_a, L0_ffn_gate_b, L0_ffn_up_a, L0_ffn_up_b, L0_ffn_down_a, L0_ffn_down_b)
    mod = (_silu(L1_c) @ L1_wmod).reshape(L1_c.shape[0], 6, 1, -1)
    sa, ca, ga, sb, cb, gb = (mod[:, 0], mod[:, 1], mod[:, 2], mod[:, 3], mod[:, 4], mod[:, 5])
    ga = (2 * (ga >= 0) - 1) * jnp.maximum(jnp.abs(ga), 0.25)
    gb = (2 * (gb >= 0) - 1) * jnp.maximum(jnp.abs(gb), 0.25)
    h = _layernorm(x, axis=-1) * (1 + ca) + sa
    x = x + ga * _L1_attn_ref(h, L1_attn_W_in, L1_attn_conv_w, L1_attn_conv_b, L1_attn_W_x, L1_attn_W_dt, L1_attn_b_dt, L1_attn_A_log, L1_attn_D, L1_attn_W_out)
    h = _layernorm(x, axis=-1) * (1 + cb) + sb
    x = x + gb * _L1_ffn_ref(h, L1_ffn_base_W, L1_ffn_router_W, L1_ffn_lora_A, L1_ffn_lora_B)
    return x

_drawn_inputs = setup_inputs


def setup_inputs(seed=0):
    import zlib

    import numpy as np

    out = dict(_drawn_inputs(seed))
    spreads = {'L1_attn_D': (1.0, 0.6)}
    factors = {'L0_attn_bias': 8.0,
     'L0_ffn_gate_a': 8.0,
     'L0_ffn_gate_b': 8.0,
     'L0_ffn_up_a': 8.0,
     'L0_ffn_up_b': 8.0,
     'L0_ffn_down_a': 8.0,
     'L0_ffn_down_b': 8.0,
     'L1_attn_W_in': 4.007,
     'L1_attn_conv_w': 3.401,
     'L1_attn_conv_b': 8.0,
     'L1_attn_W_x': 3.762,
     'L1_attn_W_dt': 8.0,
     'L1_attn_b_dt': 8.0,
     'L1_attn_A_log': 8.0,
     'L1_attn_W_out': 3.407,
     'L1_ffn_router_W': 5.074,
     'L1_ffn_lora_A': 4.37,
     'L1_ffn_lora_B': 4.352,
     'L1_ffn_base_W': 2.949}
    for name, (base, spread) in spreads.items():
        noise = np.random.default_rng([zlib.crc32(name.encode()), seed]).standard_normal(out[name].shape)
        drawn = base * np.exp(spread * noise) if base else spread * noise
        out[name] = jnp.asarray(drawn.astype(out[name].dtype))
    for name, factor in factors.items():
        out[name] = (out[name] * factor).astype(out[name].dtype)
    return out
```

```python
from contextlib import ExitStack

from concourse import mybir

F32 = mybir.dt.float32
F16 = mybir.dt.float16
I32 = mybir.dt.int32
U32 = mybir.dt.uint32
ALU = mybir.AluOpType
ACT = mybir.ActivationFunctionType
X = mybir.AxisListType.X

P = 128
T = 2048
D = 512
KD = D // P
HID = 1376
KH = -(-HID // P)
LORA = 16
NB = D // 32
CH = 256
TT = CH // P
NCH = T // CH
DI = 1024
KI = DI // P
NS = 16
RDT = 32
TAPS = 4
NE = 8
ER = NE * LORA
RA = NE + ER
WS = 64.0
DG = 4
NDG = KI // DG
STEPS = NDG * NS
LN_EPS = 1e-5
RMS_EPS = 1e-6

DTB_AT = {0: (4, 5), 1: (6, 7)}
YB_AT = {1: (4,), 2: (5,), 3: (6,), 4: (7,)}
GATE_AT = {2: (0,), 3: (1, 2), 4: (3, 4), 5: (5,), 6: (6, 7)}
T3_AT = {6: (0,), 7: (1,)}
XT_AT = {8 + m: (m,) for m in range(KI)}
WO_AT = {8 + q: (q,) for q in range(2 * TT * 2)}
YA_AT = {17 + m: (m,) for m in range(DG)}
WX_AT = 19
T4_AT = {20: (0,), 21: (1,)}
TSB_AT = 22
RA_AT = 23
DTA_AT = {24: (0, 1), 25: (2, 3)}
MID_AT = 26
BASE_AT = {28: (0,), 30: (1,)}
UB_AT = 5


def hid_rows(m):
    return min(P, HID - m * P)


def value(k, per, j):
    return k * per + (j + 1)


def build(nc, A, out):
    with ExitStack() as ctx:
        def sb(name, shape, dt=F32, c=ctx):
            return c.enter_context(nc.sbuf_tensor(name, shape, dt))

        def ps(name, shape, c):
            return c.enter_context(nc.psum_tensor(name, shape, F32))

        def sems(names, c=ctx):
            return {n: c.enter_context(nc.semaphore(n)) for n in names.split()}

        x2_dram = nc.dram_tensor("x2_scratch", (T, D), F32, kind="Internal").ap()
        bt_dram = nc.dram_tensor("bt_scratch", (NCH, 1, NS * CH), F32, kind="Internal").ap()
        mod_dram = nc.dram_tensor("mod_scratch", (4, D), F32, kind="Internal").ap()

        wi_h = sb("wi_h", [P, KD, 2 * DI], F16)
        wi_l = sb("wi_l", [P, KD, 2 * DI], F16)
        wo_h = sb("wo_h", [P, KI, D], F16)
        wo_l = sb("wo_l", [P, KI, D], F16)
        ba_h = sb("ba_h", [P, KD, D], F16)
        ba_l = sb("ba_l", [P, KD, D], F16)
        lb_h = sb("lb_h", [P, D], F16)
        lb_l = sb("lb_l", [P, D], F16)
        wx_h = sb("wx_h", [P, KI, RDT + 2 * NS], F16)
        wx_l = sb("wx_l", [P, KI, RDT + 2 * NS], F16)
        ra_h = sb("ra_h", [P, KD, RA], F16)
        ra_l = sb("ra_l", [P, KD, RA], F16)
        ident = sb("ident", [P, P])
        mhalf = sb("mhalf", [P, 8])
        W = {"wi_h": wi_h, "wi_l": wi_l, "wo_h": wo_h, "wo_l": wo_l, "ba_h": ba_h, "ba_l": ba_l, "lb_h": lb_h, "lb_l": lb_l,
             "wx_h": wx_h, "wx_l": wx_l, "ra_h": ra_h, "ra_l": ra_l, "ident": ident, "mhalf": mhalf}
        W.update(sems("const_loaded mhalf_set"))

        with ExitStack() as layer0:
            w0_h = sb("w0_h", [P, KD, D], F16, layer0)
            w0_l = sb("w0_l", [P, KD, D], F16, layer0)
            g_h = sb("g_h", [P, KD, HID], F16, layer0)
            g_l = sb("g_l", [P, KD, HID], F16, layer0)
            u_h = sb("u_h", [P, KD, HID], F16, layer0)
            u_l = sb("u_l", [P, KD, HID], F16, layer0)
            d_h = sb("d_h", [P, KH, D], F16, layer0)
            d_l = sb("d_l", [P, KH, D], F16, layer0)
            mod0 = sb("mod0", [P, 6, D], F32, layer0)
            ga_bias = sb("ga_bias", [P, D], F32, layer0)

            W0 = {"w0_h": w0_h, "w0_l": w0_l, "g_h": g_h, "g_l": g_l, "u_h": u_h, "u_l": u_l, "d_h": d_h, "d_l": d_l,
                  "mod0": mod0, "ga_bias": ga_bias}
            W0.update(W)
            with ExitStack() as c:
                setup(nc, A, mod_dram, W0, c, sb, ps, sems)
            with ExitStack() as c:
                layer_0(nc, A, x2_dram, W0, c, sb, ps, sems)
        with ExitStack() as c:
            layer_1(nc, A, x2_dram, bt_dram, mod_dram, out, W, c, sb, ps, sems)


def setup(nc, A, mod_dram, W, c, sb, ps, sems):
    stage = sb("stage", [P, 2, 2048], F32, c)
    wmod = sb("wmod", [P, 3, D], F32, c)
    lora_a = sb("lora_a", [80, HID], F32, c)
    lora_b = sb("lora_b", [80, HID], F32, c)
    cvec = sb("cvec", [P, 2, KD], F32, c)
    silu_c = sb("silu_c", [P, 2, KD], F32, c)
    silu_cb = sb("silu_cb", [P, 2, KD, P], F32, c)
    blk32 = sb("blk32", [P, P], F32, c)
    bias_b = sb("bias_b", [P, D], F32, c)
    msum = sb("msum", [P, KD * NB], F32, c)
    mon = sb("mon", [P, KD * NB], F32, c)
    gate1 = sb("gate1", [P, 2, D], F32, c)
    mod1 = sb("mod1", [P, 2, D], F32, c)
    sgn = sb("sgn", [P, D], F32, c)
    mag = sb("mag", [P, D], F32, c)
    ps_lora = ps("ps_lora", [P, 2048], c)
    ps_mod = ps("ps_mod", [P, D], c)
    ps_mask = ps("ps_mask", [P, D], c)
    S = sems("cvec_loaded silu_c_done silu_cb_done wmod_0 wmod_1 wmod_2 wmod_used mod_mm mod_step mod_done "
             "stage_0 stage_1 stage_pre stage_hi stage_lo lora_loaded lora_mm blk_loaded "
             "mask_sums mask_mm bias_loaded ga_bias_done mod_stored_0 mod_stored_1", c)
    wmod_in = (S["wmod_0"], S["wmod_1"], S["wmod_2"])
    stage_in = (S["stage_0"], S["stage_1"])
    mod_out = (S["mod_stored_0"], S["mod_stored_1"])
    KMOD = 6

    pieces = [("mask", KD * D, A["mask"], None, None, P), ("w0", KD * D, A["w0"], W["w0_h"], W["w0_l"], P)]
    for k in range(KD):
        pieces.append((("gate", k), HID, A["gate_w"][k], W["g_h"][:, k], W["g_l"][:, k], P))
    for k in range(KD):
        pieces.append((("up", k), HID, A["up_w"][k], W["u_h"][:, k], W["u_l"][:, k], P))
    for a, b in ((0, 4), (4, 8), (8, 10)):
        pieces.append((("down", a, b), (b - a) * D, A["down_w"][0:10 * P, :].rearrange("(k p) n -> p k n", p=P)[:, a:b],
                       W["d_h"][:, a:b], W["d_l"][:, a:b], P))
    pieces.append((("down", 10, 11), D, A["down_w"][10 * P:HID, :], W["d_h"][0:96, 10], W["d_l"][0:96, 10], HID - 10 * P))
    for k in range(KD):
        pieces.append((("win", k), 2 * DI, A["W_in"][k], W["wi_h"][:, k], W["wi_l"][:, k], P))
    for a in range(2):
        pieces.append((("wout", a), 4 * D, A["W_out"][:, 4 * a:4 * a + 4], W["wo_h"][:, 4 * a:4 * a + 4], W["wo_l"][:, 4 * a:4 * a + 4], P))
    pieces.append((("base",), KD * D, A["base_W"], W["ba_h"], W["ba_l"], P))
    pieces.append((("lb",), D, A["lora_B"], W["lb_h"], W["lb_l"], P))
    pieces.append((("wx",), KI * (RDT + 2 * NS), A["W_x"], W["wx_h"], W["wx_l"], P))
    pieces.append((("ra",), KD * RA, A["router_A"], W["ra_h"], W["ra_l"], P))
    mods = [(l, q) for l in range(2) for q in range(KMOD)]
    order = []
    for n, piece in enumerate(pieces):
        order.append(("piece", n))
        if n < len(mods):
            order.append(("mod", n))

    def flat(ap):
        shape = ap.shape
        return ap if len(shape) == 2 else ap.rearrange("p k n -> p (k n)")

    def hi_of(n):
        return flat(pieces[n][3][:, :, :] if len(pieces[n][3].shape) == 3 else pieces[n][3][:, :])

    def lo_of(n):
        return flat(pieces[n][4][:, :, :] if len(pieces[n][4].shape) == 3 else pieces[n][4][:, :])

    block = c.enter_context(nc.Block())
    PRE = ("w0", "gate", "up", "down", "wout", "base", "lb")

    def kind(n):
        return pieces[n][0] if isinstance(pieces[n][0], str) else pieces[n][0][0]

    pre_no = {}
    for n in range(len(pieces)):
        if kind(n) in PRE:
            pre_no[n] = len(pre_no) + 1
    lora_pieces = [n for n in range(len(pieces)) if kind(n) in ("gate", "up", "down")]

    @block.sync
    def _(sp):
        sp.dma_start(cvec[:], A["c"]).then_inc(S["cvec_loaded"], 16)
        sp.dma_start(W["ident"][:], A["ident"]).then_inc(W["const_loaded"], 16)
        sp.dma_start(blk32[:], A["blk32"]).then_inc(S["blk_loaded"], 16)
        sp.dma_start(bias_b[:], A["bias"].to_broadcast([P, D])).then_inc(S["bias_loaded"], 16)
        for r, name in enumerate(("gate", "up", "down")):
            wa, wb = (D, HID) if name != "down" else (HID, D)
            sp.dma_start(lora_a[32 * r:32 * r + LORA, 0:wa], A[name + "_a"]).then_inc(S["lora_loaded"], 16)
            sp.dma_start(lora_b[32 * r:32 * r + LORA, 0:wb], A[name + "_b"]).then_inc(S["lora_loaded"], 16)
        for what, n in order:
            if what == "piece":
                _, cols, src, _, _, rows = pieces[n]
                if n >= 2:
                    sp.wait_ge(S["stage_lo"], n - 1)
                dst = stage[0:rows, n % 2, 0:cols]
                if kind(n) == "mask":
                    dst = dst.bitcast(I32)
                if len(src.shape) == 3:
                    dst = dst.rearrange("p (k n) -> p k n", k=src.shape[1])
                sp.dma_start(dst, src).then_inc(stage_in[n % 2], 16)
            else:
                l, q = mods[n]
                for k in range(KD):
                    g = n * KD + k
                    if g >= 3:
                        sp.wait_ge(S["wmod_used"], g - 2)
                    sp.dma_start(wmod[:, g % 3, :], A[f"wmod{l}"][k * P:(k + 1) * P, q * D:(q + 1) * D])\
                      .then_inc(wmod_in[g % 3], 16)
        sp.wait_ge(mod_out[0], 32)
        sp.wait_ge(mod_out[1], 32)

    @block.tensor
    def _(pe):
        pe.wait_ge(S["silu_cb_done"], 1)
        pe.wait_ge(S["lora_loaded"], 16 * 6)
        pe.wait_ge(S["blk_loaded"], 16)
        lora_n = 0
        for what, n in order:
            if what == "mod":
                l, q = mods[n]
                if n:
                    pe.wait_ge(S["mod_done"], n)
                for k in range(KD):
                    g = n * KD + k
                    pe.wait_ge(wmod_in[g % 3], 16 * (g // 3 + 1))
                    mm = pe.matmul(ps_mod[:], silu_cb[:, l, k, :], wmod[:, g % 3, :], start=(k == 0), stop=(k == KD - 1))
                    mm.then_inc(S["wmod_used"], 1)
            elif kind(n) == "mask":
                pe.wait_ge(S["mask_sums"], 1)
                pe.matmul(ps_mask[:, 0:KD * NB], blk32[:], msum[:], start=True, stop=True).then_inc(S["mask_mm"], 1)
            elif kind(n) in ("gate", "up"):
                k = pieces[n][0][1]
                r = 32 * (kind(n) == "up")
                if lora_n:
                    pe.wait_ge(S["stage_pre"], lora_n + 1)
                for a in range(0, HID, 512):
                    b = min(HID, a + 512)
                    mm = pe.matmul(ps_lora[:, a:b], lora_a[r:r + LORA, k * P:(k + 1) * P], lora_b[r:r + LORA, a:b],
                                   start=True, stop=True)
                mm.then_inc(S["lora_mm"], 1)
                lora_n += 1
            elif kind(n) == "down":
                pe.wait_ge(S["stage_pre"], lora_n + 1)
                _, a, b = pieces[n][0]
                for k in range(a, b):
                    mm = pe.matmul(ps_lora[0:hid_rows(k), (k - a) * D:(k - a + 1) * D],
                                   lora_a[64:64 + LORA, k * P:k * P + hid_rows(k)], lora_b[64:64 + LORA, 0:D],
                                   start=True, stop=True)
                mm.then_inc(S["lora_mm"], 1)
                lora_n += 1

    @block.scalar
    def _(act):
        act.wait_ge(S["cvec_loaded"], 16)
        nc.scalar.activation(silu_c[:], cvec[:], ACT.Silu).then_inc(S["silu_c_done"], 1)
        for n in range(1, len(pieces)):
            act.wait_ge(stage_in[n % 2], 16 * (n // 2 + 1))
            if n in pre_no:
                act.wait_ge(S["stage_pre"], pre_no[n])
            rows, cols = pieces[n][5], pieces[n][1]
            nc.scalar.activation(hi_of(n), stage[0:rows, n % 2, 0:cols], ACT.Copy, scale=WS).then_inc(S["stage_hi"], 1)

    @block.gpsimd
    def _(pool):
        for j, q in enumerate((0, 1, 3, 4)):
            pool.wait_ge(S["mod_done"], KMOD + q + 1)
            pool.dma_start(mod_dram[j:j + 1, :], mod1[0:1, j % 2, :]).then_inc(mod_out[j % 2], 16)

    @block.vector
    def _(dve):
        nc.vector.memset(W["mhalf"][:], -0.5).then_inc(W["mhalf_set"], 1)
        dve.wait_ge(S["silu_c_done"], 1)
        for l in range(2):
            last = nc.vector.tensor_copy(silu_cb[:, l], silu_c[:, l, :].unsqueeze(2).to_broadcast([P, KD, P]))
        last.then_inc(S["silu_cb_done"], 1)
        step = 0
        pre = 0
        lora = 0
        row = 0

        def split_low(n):
            rows, cols = pieces[n][5], pieces[n][1]
            dve.wait_ge(S["stage_hi"], n)
            nc.vector.scalar_tensor_tensor(lo_of(n), stage[0:rows, n % 2, 0:cols], WS, hi_of(n), ALU.mult, ALU.subtract)\
              .then_inc(S["stage_lo"], 1)

        for what, n in order:
            if what == "mod":
                l, q = mods[n]
                dve.wait_ge(S["wmod_used"], KD * (n + 1))
                if q in (2, 5):
                    dst = W["mod0"][:, q, :] if l == 0 else gate1[:, q // 3, :]
                    nc.vector.tensor_scalar(sgn[:], ps_mod[:], 0.0, 2.0, ALU.is_ge, ALU.mult).then_inc(S["mod_step"], 1)
                    nc.vector.tensor_copy(mag[:], ps_mod[:]).then_inc(S["mod_step"], 1)
                    step += 2
                    dve.wait_ge(S["mod_step"], step)
                    nc.vector.scalar_tensor_tensor(mag[:], mag[:], -1.0, mag[:], ALU.mult, ALU.max).then_inc(S["mod_step"], 1)
                    step += 1
                    dve.wait_ge(S["mod_step"], step)
                    nc.vector.tensor_scalar(mag[:], mag[:], 0.25, 1.0 / WS if l == 0 else 1.0, ALU.max, ALU.mult)\
                      .then_inc(S["mod_step"], 1)
                    step += 1
                    dve.wait_ge(S["mod_step"], step)
                    nc.vector.scalar_tensor_tensor(dst, sgn[:], 1.0, mag[:], ALU.subtract, ALU.mult).then_inc(S["mod_done"], 1)
                    if (l, q) == (0, 2):
                        dve.wait_ge(S["mod_done"], n + 1)
                        dve.wait_ge(S["bias_loaded"], 16)
                        nc.vector.scalar_tensor_tensor(W["ga_bias"][:], dst, WS, bias_b[:], ALU.mult, ALU.mult)\
                          .then_inc(S["ga_bias_done"], 1)
                        dve.wait_ge(S["ga_bias_done"], 1)
                else:
                    if l:
                        if row >= 2:
                            dve.wait_ge(mod_out[row % 2], 16)
                        dst = mod1[:, row % 2, :]
                        row += 1
                    else:
                        dst = W["mod0"][:, q, :]
                    nc.vector.tensor_scalar(dst, ps_mod[:], 1.0 if q in (1, 4) else 0.0, None, ALU.add)\
                      .then_inc(S["mod_done"], 1)
                continue
            dve.wait_ge(stage_in[n % 2], 16 * (n // 2 + 1))
            rows, cols = pieces[n][5], pieces[n][1]
            st = stage[0:rows, n % 2, 0:cols]
            if kind(n) == "mask":
                nc.vector.tensor_reduce(msum[:], st.bitcast(I32).rearrange("p (b w) -> p b w", w=32), X, ALU.add)\
                  .then_inc(S["mask_sums"], 1)
                dve.wait_ge(S["mask_mm"], 1)
                nc.vector.tensor_scalar(mon[:], ps_mask[:, 0:KD * NB], 0.0, None, ALU.is_gt).then_inc(S["stage_lo"], 1)
                dve.wait_ge(S["stage_lo"], 1)
                continue
            if kind(n) == "w0":
                blocks = st.rearrange("p (b w) -> p b w", w=32)
                nc.vector.tensor_tensor(blocks, blocks, mon[:].unsqueeze(2).to_broadcast([P, KD * NB, 32]), ALU.mult)\
                  .then_inc(S["stage_pre"], 1)
            elif kind(n) in ("gate", "up", "down"):
                lora += 1
                dve.wait_ge(S["lora_mm"], lora)
                nc.vector.tensor_tensor(st, st, ps_lora[0:rows, 0:cols], ALU.add).then_inc(S["stage_pre"], 1)
            elif kind(n) in ("wout", "base", "lb"):
                q = 2 if kind(n) == "wout" else 5
                dve.wait_ge(S["mod_done"], KMOD + q + 1)
                g = gate1[:, q // 3, :]
                if kind(n) == "lb":
                    nc.vector.tensor_tensor(st, st, g, ALU.mult).then_inc(S["stage_pre"], 1)
                else:
                    v = st.rearrange("p (k n) -> p k n", n=D)
                    nc.vector.tensor_tensor(v, v, g.unsqueeze(1).to_broadcast([P, 4, D]), ALU.mult).then_inc(S["stage_pre"], 1)
            split_low(n)
        dve.wait_ge(S["stage_lo"], len(pieces))


def products(pe, out, left, right, first=True, last=True):
    n = len(left)
    for k, ((lh, ll), (rh, rl)) in enumerate(zip(left, right)):
        pe.matmul(out, lh, rh, start=(first and k == 0), stop=False)
        pe.matmul(out, lh, rl, start=False, stop=False)
        mm = pe.matmul(out, ll, rh, start=False, stop=(last and k == n - 1))
    return mm


def layer_0(nc, A, x2_dram, W, c, sb, ps, sems):
    xa = sb("xa", [P, TT, D], F32, c)
    xb = sb("xb", [P, TT, D], F32, c)
    x1 = sb("x1", [P, TT, D], F32, c)
    x1r = sb("x1r", [P, TT, D], F32, c)
    scaled = sb("scaled", [P, D], F32, c)
    h1_h = sb("h1_h", [P, KD, CH], F16, c)
    h1_l = sb("h1_l", [P, KD, CH], F16, c)
    h2_h = sb("h2_h", [P, KD, CH], F16, c)
    h2_l = sb("h2_l", [P, KD, CH], F16, c)
    hid_h = sb("hid_h", [P, KH, CH], F16, c)
    hid_l = sb("hid_l", [P, KH, CH], F16, c)
    RING = 3
    sil = sb("sil", [P, RING, CH], F32, c)
    hid = sb("hid", [P, RING, CH], F32, c)
    stats = sb("stats", [P, TT, 6], F32, c)
    mv = sb("mv", [P, TT, 2], F32, c)
    veps = sb("veps", [P, TT], F32, c)
    rstd = sb("rstd", [P, TT], F32, c)
    ps_t = ps("ps_t", [P, TT, KD, P], c)
    ps_gu = ps("ps_gu", [P, 4, 2, CH], c)
    ps_o = ps("ps_o", [P, TT, D], c)
    S = sems("x_loaded xb_done stats_done aggr_done veps_done rstd_done norm_done scale_done shift_done t_mm t_hi t_lo "
             "lin_mm o_used x1_done x1r_done gu_mm sil_done hid_done hid_hi hid_lo down_mm x2_done x2_stored met_dve met_pool", c)
    GU_LAG, HID_LAG = 3, 2
    x_v = A["x"].rearrange("(c t p) d -> c p t d", p=P, t=TT)
    x2_v = x2_dram.rearrange("(c t p) d -> c p t d", p=P, t=TT)
    sa, ca, ga, sb_, cb, gb = (W["mod0"][:, q, :] for q in range(6))
    T1_AFTER, LIN_AFTER = 3, 6
    block = c.enter_context(nc.Block())


    @block.sync
    def _(sp):
        sp.dma_start(xa[:], x_v[0]).then_inc(S["x_loaded"], 16)

        def chunk(k):
            sp.wait_ge(S["t_mm"], value(k, 4, 3))
            sp.dma_start(xa[:], x_v[k + 1]).then_inc(S["x_loaded"], 16)

        def store(k):
            sp.wait_ge(S["x2_done"], value(k, TT, 1))
            sp.dma_start(x2_v[k], x1r[:]).then_inc(S["x2_stored"], 16)

        with sp.Fori(0, NCH - 1) as k:
            chunk(k)
            store(k)
        store(NCH - 1)
        sp.wait_ge(S["x2_stored"], 16 * NCH)

    @block.tensor
    def _(pe):
        pe.wait_ge(W["const_loaded"], 16)

        def turn(e):
            for t in range(TT):
                pe.wait_ge(S["shift_done"], e + 1)
                pe.wait_ge(S["t_lo"], e * TT + (t + 1))
                for k in range(KD):
                    tr = pe.transpose(ps_t[:, t, k], xa[:, t, k * P:(k + 1) * P], W["ident"][:])
                tr.then_inc(S["t_mm"], 1)

        def linear(n, first):
            for t in range(TT):
                pe.wait_ge(S["t_lo"], n * (2 * TT) + (TT + TT))
                if not first:
                    pe.wait_ge(S["o_used"], n * (2 * TT) + (t - 3))
                tok = slice(t * P, (t + 1) * P)
                products(pe, ps_o[:, t], [(h1_h[:, k, tok], h1_l[:, k, tok]) for k in range(KD)],
                         [(W["w0_h"][:, k], W["w0_l"][:, k]) for k in range(KD)]).then_inc(S["lin_mm"], 1)

        def gate_up(k, m):
            rows = hid_rows(m)
            cols = slice(m * P, m * P + rows)
            if m == 0:
                pe.wait_ge(S["t_lo"], k * (2 * TT) + (TT + 2 * TT))
            pe.wait_ge(S["hid_done"], k * KH + (m + 1))
            dst = ps_gu[0:rows, m % 4]
            right = [(h2_h[:, i], h2_l[:, i]) for i in range(KD)]
            products(pe, dst[:, 0], [(W["g_h"][:, i, cols], W["g_l"][:, i, cols]) for i in range(KD)], right)
            products(pe, dst[:, 1], [(W["u_h"][:, i, cols], W["u_l"][:, i, cols]) for i in range(KD)], right)\
                .then_inc(S["gu_mm"], 1)

        def down(k, t, last):
            pe.wait_ge(S["hid_lo"], k * KH + (KH + HID_LAG))
            pe.wait_ge(S["o_used"], k * (2 * TT) + ((1 if last else 3) + t))
            tok = slice(t * P, (t + 1) * P)
            left = [(hid_h[0:hid_rows(m), m, tok], hid_l[0:hid_rows(m), m, tok]) for m in range(KH)]
            right = [(W["d_h"][0:hid_rows(m), m], W["d_l"][0:hid_rows(m), m]) for m in range(KH)]
            products(pe, ps_o[:, t], left, right).then_inc(S["down_mm"], 1)

        turn(0)
        linear(0, True)
        turn(1)
        with pe.Fori(0, NCH - 1) as k:
            for m in range(KH):
                gate_up(k, m)
                if m == T1_AFTER:
                    turn(k * 2 + 2)
                if m == LIN_AFTER:
                    linear(k + 1, False)
            down(k, 0, False)
            turn(k * 2 + 3)
            down(k, 1, False)
        for m in range(KH):
            gate_up(NCH - 1, m)
        for t in range(TT):
            down(NCH - 1, t, True)

    @block.scalar
    def _(act):
        def high(e, dst):
            for t in range(TT):
                act.wait_ge(S["t_mm"], e * TT + (t + 1))
                nc.scalar.activation(dst[:, :, t * P:(t + 1) * P], ps_t[:, t], ACT.Copy).then_inc(S["t_hi"], 1)

        def silu(k, m):
            rows = hid_rows(m)
            act.wait_ge(S["gu_mm"], value(k, KH, m))
            act.wait_ge(S["hid_done"], k * KH + (m + GU_LAG - HID_LAG + 1))
            nc.scalar.activation(sil[0:rows, m % RING], ps_gu[0:rows, m % 4, 0], ACT.Silu, scale=1.0 / WS)\
              .then_inc(S["sil_done"], 1)

        def hidden_high(k, m):
            rows = hid_rows(m)
            act.wait_ge(S["hid_done"], k * KH + (m + GU_LAG + 1))
            if m == 0:
                act.wait_ge(S["down_mm"], k * TT + TT)
            nc.scalar.activation(hid_h[0:rows, m], hid[0:rows, m % RING], ACT.Copy).then_inc(S["hid_hi"], 1)

        def gate_ups(k, last):
            for m in range(KH):
                silu(k, m)
                if m:
                    hidden_high(k, m - 1)
                if m == T1_AFTER and not last:
                    high(k * 2 + 2, h1_h)
            hidden_high(k, KH - 1)

        high(0, h1_h)
        high(1, h2_h)
        with act.Fori(0, NCH - 1) as k:
            gate_ups(k, False)
            high(k * 2 + 3, h2_h)
        gate_ups(NCH - 1, True)

    @block.gpsimd
    def _(pool):
        pool.wait_ge(W["mhalf_set"], 1)
        pool.sem_inc(S["hid_lo"], HID_LAG)

        def add_bias(n, first):
            pool.wait_ge(S["x_loaded"], n * 16 + 16)
            if not first:
                pool.wait_ge(S["x1_done"], n * TT)
            nc.gpsimd.tensor_tensor(xb[:], xa[:], W["ga_bias"][:].unsqueeze(1).to_broadcast([P, TT, D]), ALU.add)\
              .then_inc(S["xb_done"], 1)

        def inv_std(e):
            pool.wait_ge(S["aggr_done"], e * TT + TT)
            pool.sem_inc(S["met_pool"], 1)
            nc.gpsimd.tensor_scalar(veps[:], mv[:, :, 1], LN_EPS, None, ALU.add).then_inc(S["veps_done"], 1)
            pool.wait_ge(S["veps_done"], e + 1)
            nc.gpsimd.tensor_tensor(rstd[:], veps[:], W["mhalf"][:, 0:TT], ALU.pow).then_inc(S["rstd_done"], 1)

        def modulate(e, scale, shift):
            pool.wait_ge(S["norm_done"], e * TT + TT)
            nc.gpsimd.tensor_tensor(xa[:], xa[:], scale.unsqueeze(1).to_broadcast([P, TT, D]), ALU.mult).then_inc(S["scale_done"], 1)
            pool.wait_ge(S["scale_done"], e + 1)
            nc.gpsimd.tensor_tensor(xa[:], xa[:], shift.unsqueeze(1).to_broadcast([P, TT, D]), ALU.add).then_inc(S["shift_done"], 1)

        def hidden_low(k, m):
            rows = hid_rows(m)
            pool.wait_ge(S["hid_hi"], value(k, KH, m))
            nc.gpsimd.tensor_tensor(hid_l[0:rows, m], hid[0:rows, m % RING], hid_h[0:rows, m], ALU.subtract)\
              .then_inc(S["hid_lo"], 1)

        def keep_x1(n, first):
            pool.wait_ge(S["x1_done"], n * TT + TT)
            if not first:
                pool.wait_ge(S["x2_stored"], n * 16)
            pool.sem_inc(S["met_pool"], 1)
            nc.gpsimd.tensor_copy(x1r[:], x1[:]).then_inc(S["x1r_done"], 1)

        add_bias(0, True)
        inv_std(0)
        modulate(0, ca, sa)
        inv_std(1)
        modulate(1, cb, sb_)
        keep_x1(0, True)
        with pool.Fori(0, NCH - 1) as k:
            for m in range(KH):
                hidden_low(k, m)
                if m == 0:
                    add_bias(k + 1, False)
                    inv_std(k * 2 + 2)
                if m == 1:
                    modulate(k * 2 + 2, ca, sa)
                if m == LIN_AFTER:
                    inv_std(k * 2 + 3)
                if m == LIN_AFTER + 1:
                    modulate(k * 2 + 3, cb, sb_)
            keep_x1(k + 1, False)
        for m in range(KH):
            hidden_low(NCH - 1, m)

    @block.vector
    def _(dve):
        dve.sem_inc(S["t_lo"], TT)
        dve.sem_inc(S["hid_done"], GU_LAG)
        dve.sem_inc(S["down_mm"], TT)

        def statistics(e, src):
            for t in range(TT):
                nc.vector.bn_stats(stats[:, t], src[:, t]).then_inc(S["stats_done"], 1)
            for t in range(TT):
                dve.wait_ge(S["stats_done"], e * TT + (t + 1))
                dve.sem_inc(S["met_dve"], 1)
                nc.vector.bn_aggr(mv[:, t], stats[:, t]).then_inc(S["aggr_done"], 1)

        def normalise(e, src):
            dve.wait_ge(S["rstd_done"], e + 1)
            for t in range(TT):
                nc.vector.tensor_scalar(xa[:, t], src[:, t], mv[:, t, 0:1], rstd[:, t:t + 1], ALU.subtract, ALU.mult)\
                  .then_inc(S["norm_done"], 1)

        def low(e, hi, lo):
            for t in range(TT):
                tok = slice(t * P, (t + 1) * P)
                dve.wait_ge(S["t_hi"], e * TT + (t + 1))
                nc.vector.tensor_tensor(lo[:, :, tok], ps_t[:, t], hi[:, :, tok], ALU.subtract).then_inc(S["t_lo"], 1)

        def hidden(k, m):
            rows = hid_rows(m)
            dve.wait_ge(S["sil_done"], value(k, KH, m))
            dve.wait_ge(S["hid_lo"], k * KH + (m + 1))
            nc.vector.scalar_tensor_tensor(hid[0:rows, m % RING], ps_gu[0:rows, m % 4, 1], 1.0 / WS,
                                           sil[0:rows, m % RING], ALU.mult, ALU.mult).then_inc(S["hid_done"], 1)

        def add_linear(n, first):
            for t in range(TT):
                dve.wait_ge(S["lin_mm"], n * TT + (t + 1))
                nc.vector.tensor_tensor(scaled[:], ps_o[:, t], ga, ALU.mult).then_inc(S["o_used"], 1)
                if first:
                    dve.wait_ge(S["o_used"], t + 1)
                else:
                    dve.wait_ge(S["o_used"], n * (2 * TT) + (t + 1 - TT))
                    dve.wait_ge(S["x1r_done"], n)
                dve.wait_ge(S["xb_done"], n + 1)
                nc.vector.tensor_tensor(x1[:, t], scaled[:], xb[:, t], ALU.add).then_inc(S["x1_done"], 1)
                dve.wait_ge(S["x1_done"], n * TT + (t + 1))

        def add_swiglu(k, t, last):
            dve.wait_ge(S["down_mm"], k * TT + (t + 1 + TT))
            nc.vector.tensor_tensor(scaled[:], ps_o[:, t], gb, ALU.mult).then_inc(S["o_used"], 1)
            dve.wait_ge(S["o_used"], k * (2 * TT) + ((3 if last else 5) + t))
            dve.wait_ge(S["x1r_done"], k + 1)
            nc.vector.tensor_tensor(x1r[:, t], scaled[:], x1r[:, t], ALU.add).then_inc(S["x2_done"], 1)
            dve.wait_ge(S["x2_done"], value(k, TT, t))

        dve.wait_ge(S["x_loaded"], 16)
        statistics(0, xa)
        dve.wait_ge(S["xb_done"], 1)
        normalise(0, xa)
        low(0, h1_h, h1_l)
        add_linear(0, True)
        statistics(1, x1)
        normalise(1, x1)
        low(1, h2_h, h2_l)
        with dve.Fori(0, NCH - 1) as k:
            for m in range(KH):
                hidden(k, m)
                if m == 0:
                    dve.wait_ge(S["x_loaded"], (k + 1) * 16 + 16)
                    statistics(k * 2 + 2, xa)
                if m == 1:
                    dve.wait_ge(S["xb_done"], k + 2)
                    normalise(k * 2 + 2, xa)
                if m == T1_AFTER:
                    low(k * 2 + 2, h1_h, h1_l)
                if m == LIN_AFTER:
                    add_linear(k + 1, False)
                    statistics(k * 2 + 3, x1)
                if m == LIN_AFTER + 1:
                    normalise(k * 2 + 3, x1)
            add_swiglu(k, 0, False)
            low(k * 2 + 3, h2_h, h2_l)
            add_swiglu(k, 1, False)
        for m in range(KH):
            hidden(NCH - 1, m)
        for t in range(TT):
            add_swiglu(NCH - 1, t, True)


def layer_1(nc, A, x2_dram, bt_dram, mod_dram, out, W, c, sb, ps, sems):
    xa = sb("xn", [P, TT, D], F32, c)
    x3 = sb("x3", [P, TT, D], F32, c)
    mod = sb("mod", [P, 4, D], F32, c)
    h3_h = sb("h3_h", [P, KD, CH], F16, c)
    h3_l = sb("h3_l", [P, KD, CH], F16, c)
    taps_raw = sb("taps_raw", [P, KI, TAPS + 1], F32, c)
    taps = sb("taps", [P, KI, TAPS + 1], F32, c)
    d_vec = sb("d_vec", [P, KI], F32, c)
    diag_d = sb("diag_d", [P, KI, P], F32, c)
    b_dt = sb("b_dt", [P, KI], F32, c)
    w_dt = sb("w_dt", [RDT, DI], F32, c)
    a_log = sb("a_log", [P, KI, NS], F32, c)
    a_exp = sb("a_exp", [P, KI, NS], F32, c)
    a_neg = sb("a_neg", [P, KI, NS], F32, c)
    expert = sb("expert", [P, NE], F32, c)
    hist = sb("hist", [P, KI, TAPS - 1], F32, c)
    xw = sb("xw", [P, 2, TAPS - 1 + CH], F32, c)
    cv = sb("cv", [P, 2, CH], F32, c)
    th = sb("th", [P, 2, CH], F32, c)
    u = sb("u", [P, KI, CH], F32, c)
    u_h = sb("uu_h", [P, KI, CH], F16, c)
    u_l = sb("uu_l", [P, KI, CH], F16, c)
    h4_h = u_h[:, 0:KD]
    h4_l = u_h[:, KD:2 * KD]
    ssm = sb("ssm", [P, TT, RDT + 2 * NS], F32, c)
    ssq = sb("ssq", [P, TT, RDT + 2 * NS], F32, c)
    ssn = sb("ssn", [P, TT, RDT + 2 * NS], F32, c)
    c_cur = sb("c_cur", [P, TT, NS], F32, c)
    msq = sb("msq", [P, TT, 3], F32, c)
    mse = sb("mse", [P, TT, 3], F32, c)
    rms = sb("rms", [P, TT, 3], F32, c)
    tsb = sb("tsb", [RDT + NS, CH], F32, c)
    b_all = sb("b_all", [P, NS, CH], F32, c)
    ab = sb("ab", [P, DG, CH], F32, c)
    dt = sb("dt", [P, KI, CH], F32, c)
    dtu = sb("dtu", [P, KI, CH], F32, c)
    sg = sb("sg", [P, KI, CH], F32, c)
    da = sb("da", [P, 2, DG, CH], F32, c)
    dbu = sb("dbu", [P, 2, DG, CH], F32, c)
    h = sb("h", [P, 2, DG, CH], F32, c)
    carry = sb("carry", [P, STEPS, DG], F32, c)
    acc = sb("acc", [P, TT, DI], F32, c)
    y32 = sb("y32", [P, 2, CH], F32, c)
    y_h = sb("y_h", [P, KI, CH], F16, c)
    y_l = sb("y_l", [P, KI, CH], F16, c)
    stats = sb("stats1", [P, TT, 6], F32, c)
    mv = sb("mv1", [P, TT, 2], F32, c)
    veps = sb("veps1", [P, TT], F32, c)
    rstd = sb("rstd1", [P, TT], F32, c)
    rl = sb("rl", [P, TT, RA], F32, c)
    top = sb("top", [P, TT, 8], F32, c)
    top_at = sb("top_at", [P, TT, 8], U32, c)
    at = sb("at", [P, TT, 2], F32, c)
    gap = sb("gap", [P, TT], F32, c)
    e2 = sb("e2", [P, TT], F32, c)
    e2p = sb("e2p", [P, TT], F32, c)
    inv = sb("inv", [P, TT], F32, c)
    w12 = sb("w12", [P, TT, 2], F32, c)
    wd = sb("wd", [P, 2, TT, NE], F32, c)
    mid = sb("mid", [P, TT, ER], F32, c)
    mid_h = sb("mid_h", [P, TT, P], F16, c)
    mid_l = sb("mid_l", [P, TT, P], F16, c)
    ps_h = ps("ps_h", [P, 2, TT, D], c)
    ps_m = ps("ps_m", [P, 2, D], c)
    ps_s = ps("ps_s", [P, D], c)
    ps_o = ps("ps_o1", [P, D], c)
    S = sems("w1_loaded taps_done diag_done aexp_done aneg_done zeros_done mod_loaded "
             "xa_loaded x3_loaded stats_a aggr_a veps_a rstd_a norm_a scale_a shift_a "
             "stats_b aggr_b veps_b rstd_b norm_b scale_b shift_b "
             "t3_mm t3_hi t3_lo gate_mm gate_th gate_sg x_mm xw_done conv_done tanh_done u_done u_hi u_lo wx_mm "
             "ssm_done sq_done ms_done me_done rms_done ssn_done tsb_mm tsb_done bt_stored b_0 b_1 b_2 b_3 "
             "dt_mm dt_abs dt_max dt_exp dt_ln dt_done dtu_done c_done "
             "exp_done dbu_done scan_done carry_done hT_done hT_used "
             "y_mm y_done y_hi y_lo wo_mm x3_done t4_mm t4_hi t4_lo ra_mm rl_done "
             "top_done top_at_done at_done gap_done e2_done e2p_done inv_done w1_done w2_done m1_done m2_done wd_done "
             "mid_done mid_mm mid_hi mid_lo base_mm out_done out_stored met_dve met_pe met_pool", c)
    b_in = (S["b_0"], S["b_1"], S["b_2"], S["b_3"])
    BQ = NS // 4
    LASTC = NCH - 1
    USES = STEPS + NDG
    x2_v = x2_dram.rearrange("(c t p) d -> c p t d", p=P, t=TT)
    out_v = out.rearrange("a (c t p) d -> c p (a t) d", p=P, t=TT)

    def use_of_step(s):
        return s + 1 + (s >= UB_AT)

    block = c.enter_context(nc.Block())

    @block.sync
    def _(sp):
        sp.dma_start(taps_raw[:], A["conv"]).then_inc(S["w1_loaded"], 16)
        sp.dma_start(d_vec[:], A["D"]).then_inc(S["w1_loaded"], 16)
        sp.dma_start(b_dt[:], A["b_dt"]).then_inc(S["w1_loaded"], 16)
        sp.dma_start(w_dt[:], A["W_dt"]).then_inc(S["w1_loaded"], 16)
        sp.dma_start(a_log[:], A["A_log"]).then_inc(S["w1_loaded"], 16)
        sp.dma_start(expert[:], A["expert"]).then_inc(S["w1_loaded"], 16)
        for j in range(4):
            sp.dma_start(mod[:, j, :], mod_dram[j:j + 1, :].to_broadcast([P, D])).then_inc(S["mod_loaded"], 16)

        def load_xa(n):
            sp.dma_start(xa[:], x2_v[n]).then_inc(S["xa_loaded"], 16)

        def spread_b(n, first):
            sp.wait_ge(S["tsb_done"], n + 1)
            sp.dma_start(bt_dram[n].rearrange("a (s t) -> (a s) t", s=NS), tsb[RDT:RDT + NS, :]).then_inc(S["bt_stored"], 16)
            sp.wait_ge(S["bt_stored"], n * 16 + 16)
            for q in range(4):
                if not first:
                    sp.wait_ge(S["dbu_done"], (n - 1) * STEPS + (NS + BQ * q + BQ))
                sp.dma_start(b_all[:, BQ * q:BQ * q + BQ, :],
                             bt_dram[n][:, BQ * q * CH:(BQ * q + BQ) * CH].to_broadcast([P, BQ * CH])
                             .rearrange("p (s t) -> p s t", s=BQ)).then_inc(b_in[q], 16)

        def iteration(i, p, n, first, second):
            if n is not None:
                if first or second:
                    sp.wait_ge(S["t3_mm"], n * TT)
                else:
                    sp.wait_ge(S["t4_mm"], p * TT)
                load_xa(n)
            if p is not None:
                if not second:
                    sp.wait_ge(S["out_stored"], p * 16)
                sp.dma_start(x3[:], x2_v[p]).then_inc(S["x3_loaded"], 16)
            if n is not None:
                spread_b(n, False)
            if p is not None:
                store(p)

        def store(p):
            sp.wait_ge(S["out_done"], value(p, TT, 1))
            sp.dma_start(out_v[p], x3[:]).then_inc(S["out_stored"], 16)

        load_xa(0)
        spread_b(0, True)
        iteration(0, None, 1, True, False)
        iteration(1, 0, 2, False, True)
        with sp.Fori(2, LASTC) as i:
            iteration(i, i - 1, i + 1, False, False)
        iteration(LASTC, LASTC - 1, None, False, False)
        sp.wait_ge(S["out_stored"], LASTC * 16)
        sp.dma_start(x3[:], x2_v[LASTC]).then_inc(S["x3_loaded"], 16)
        store(LASTC)
        sp.wait_ge(S["out_stored"], NCH * 16)

    @block.tensor
    def _(pe):
        last_s = [None]

        def take_s(sem, val):
            if last_s[0] is not None:
                pe.wait_ge(*last_s[0])
            last_s[0] = (sem, val)

        def turn_in(n, t, t_mm, shift, lo):
            take_s(lo, n * TT + (t + 1))
            pe.wait_ge(shift, n + 1)
            for k in range(KD):
                tr = pe.transpose(ps_s[:, k * P:(k + 1) * P], xa[:, t, k * P:(k + 1) * P], W["ident"][:])
            tr.then_inc(t_mm, 1)

        h3 = [(h3_h[:, k], h3_l[:, k]) for k in range(KD)]

        def x_tile(n, m, first):
            if m < 2:
                if not first:
                    pe.wait_ge(S["gate_sg"], (n - 1) * KI + (KI - 1 + m))
            else:
                pe.wait_ge(S["xw_done"], n * (3 * KI) + 3 * (m - 1))
            if m == 0:
                pe.wait_ge(S["t3_lo"], n * TT + TT)
            cols = slice(m * P, (m + 1) * P)
            products(pe, ps_m[:, m % 2, 0:CH], [(W["wi_h"][:, k, cols], W["wi_l"][:, k, cols]) for k in range(KD)], h3)\
                .then_inc(S["x_mm"], 1)

        def gate_tile(i, m):
            if m < 2:
                pe.wait_ge(S["dt_max"], i * KI + (DG + 2 + m + 1))
                pe.wait_ge(S["dt_abs"], i * KI + (DG + 2 + m + 1))
            else:
                pe.wait_ge(S["gate_sg"], i * KI + (m - 1))
            cols = slice(DI + m * P, DI + (m + 1) * P)
            products(pe, ps_m[:, m % 2, 0:CH], [(W["wi_h"][:, k, cols], W["wi_l"][:, k, cols]) for k in range(KD)], h3)\
                .then_inc(S["gate_mm"], 1)

        def dt_tile(n, m):
            if m < 2:
                pe.wait_ge(S["xw_done"], n * (3 * KI) + 3 * (KI - 1 + m))
            else:
                pe.wait_ge(S["dt_max"], n * KI + (m - 1))
                pe.wait_ge(S["dt_abs"], n * KI + (m - 1))
            if m == 0:
                pe.wait_ge(S["tsb_done"], n + 1)
            pe.matmul(ps_m[:, m % 2, 0:CH], w_dt[:, m * P:(m + 1) * P], tsb[0:RDT, :], start=True, stop=True)\
                .then_inc(S["dt_mm"], 1)

        def wx(n):
            take_s(S["ssm_done"], n + 1)
            pe.wait_ge(S["u_lo"], n * KI + KI)
            for t in range(TT):
                tok = slice(t * P, (t + 1) * P)
                mm = products(pe, ps_s[:, t * 64:(t + 1) * 64], [(u_h[:, k, tok], u_l[:, k, tok]) for k in range(KI)],
                              [(W["wx_h"][:, k], W["wx_l"][:, k]) for k in range(KI)])
            mm.then_inc(S["wx_mm"], 1)

        def turn_tsb(n):
            take_s(S["tsb_done"], n + 1)
            pe.wait_ge(S["ssn_done"], n * 2 + 2)
            pe.sem_inc(S["met_pe"], 1)
            for t in range(TT):
                tr = pe.transpose(ps_s[0:RDT + NS, t * P:(t + 1) * P], ssn[:, t, 0:RDT + NS], W["ident"][:])
            tr.then_inc(S["tsb_mm"], 1)

        def h_bank(i, use, first):
            if not (first and use < 2):
                pe.wait_ge(S["hT_used"], i * USES + (use - 1))
            return use % 2

        def init_acc(i, g, first):
            b = h_bank(i, 0 if g == 0 else UB_AT + 1, first)
            if g == 0:
                pe.wait_ge(S["u_done"], i * KI + KI)
            for t in range(TT):
                for j in range(DG):
                    mm = pe.matmul(ps_h[:, b, t, j * P:(j + 1) * P], u[:, g * DG + j, t * P:(t + 1) * P],
                                   diag_d[:, g * DG + j, :], start=True, stop=True)
            mm.then_inc(S["hT_done"], 1)

        def turn_h(i, s, first):
            b = h_bank(i, use_of_step(s), first)
            pe.wait_ge(S["scan_done"], value(i, STEPS, s))
            for t in range(TT):
                for j in range(DG):
                    tr = pe.transpose(ps_h[:, b, t, j * P:(j + 1) * P], h[:, s % 2, j, t * P:(t + 1) * P], W["ident"][:])
            tr.then_inc(S["hT_done"], 1)

        def turn_y(i, m):
            take_s(S["y_done"], value(i, KI, m))
            if m % DG == 0:
                last = use_of_step(NS - 1) if m == 0 else USES - 1
                pe.wait_ge(S["hT_used"], i * USES + (last + 1))
            for t in range(TT):
                tr = pe.transpose(ps_s[:, t * P:(t + 1) * P], acc[:, t, m * P:(m + 1) * P], W["ident"][:])
            tr.then_inc(S["y_mm"], 1)

        def out_projection(p, q, first):
            t, part = q // 4, q % 4
            if q == 0:
                pe.wait_ge(S["y_lo"], p * KI + KI)
                if not first:
                    pe.wait_ge(S["out_done"], p * TT)
            if q == 4:
                pe.wait_ge(S["x3_done"], p * TT + 1)
            tok = slice(t * P, (t + 1) * P)
            ks = range(2 * part, 2 * part + 2)
            mm = products(pe, ps_o[:], [(y_h[:, k, tok], y_l[:, k, tok]) for k in ks],
                          [(W["wo_h"][:, k], W["wo_l"][:, k]) for k in ks], part == 0, part == 3)
            if part == 3:
                mm.then_inc(S["wo_mm"], 1)

        def router(p):
            take_s(S["rl_done"], p + 1)
            for t in range(TT):
                tok = slice(t * P, (t + 1) * P)
                mm = products(pe, ps_s[:, t * RA:(t + 1) * RA], [(h4_h[:, k, tok], h4_l[:, k, tok]) for k in range(KD)],
                              [(W["ra_h"][:, k], W["ra_l"][:, k]) for k in range(KD)])
            mm.then_inc(S["ra_mm"], 1)

        def turn_mid(p):
            take_s(S["mid_lo"], p + 1)
            pe.wait_ge(S["mid_done"], p + 1)
            for t in range(TT):
                tr = pe.transpose(ps_s[:, t * P:(t + 1) * P], mid[:, t, :], W["ident"][:])
            tr.then_inc(S["mid_mm"], 1)

        def experts(p, t):
            pe.wait_ge(S["x3_done"] if t == 0 else S["out_done"], p * TT + (TT if t == 0 else 1))
            pe.wait_ge(S["mid_lo"], p + 1)
            tok = slice(t * P, (t + 1) * P)
            products(pe, ps_o[:], [(h4_h[:, k, tok], h4_l[:, k, tok]) for k in range(KD)] + [(mid_h[:, t], mid_l[:, t])],
                     [(W["ba_h"][:, k], W["ba_l"][:, k]) for k in range(KD)] + [(W["lb_h"][:], W["lb_l"][:])]).then_inc(S["base_mm"], 1)

        def iteration(i, p, n, first, second):
            for s in range(STEPS):
                if s == 0:
                    init_acc(i, 0, first)
                if s == UB_AT:
                    init_acc(i, 1, first)
                turn_h(i, s, first)
                for m in DTB_AT.get(s, ()):
                    dt_tile(i, m)
                if p is not None:
                    for m in YB_AT.get(s, ()):
                        turn_y(p, m)
                for m in GATE_AT.get(s, ()):
                    gate_tile(i, m)
                if n is not None:
                    for t in T3_AT.get(s, ()):
                        turn_in(n, t, S["t3_mm"], S["shift_a"], S["t3_lo"])
                    for m in XT_AT.get(s, ()):
                        x_tile(n, m, False)
                if p is not None:
                    for q in WO_AT.get(s, ()):
                        out_projection(p, q, second)
                for m in YA_AT.get(s, ()):
                    turn_y(i, m)
                if n is not None and s == WX_AT:
                    wx(n)
                if p is not None:
                    for t in T4_AT.get(s, ()):
                        turn_in(p, t, S["t4_mm"], S["shift_b"], S["t4_lo"])
                if n is not None and s == TSB_AT:
                    turn_tsb(n)
                if p is not None and s == RA_AT:
                    pe.wait_ge(S["t4_lo"], p * TT + TT)
                    router(p)
                if n is not None:
                    for m in DTA_AT.get(s, ()):
                        dt_tile(n, m)
                if p is not None and s == MID_AT:
                    turn_mid(p)
                if p is not None:
                    for t in BASE_AT.get(s, ()):
                        experts(p, t)

        pe.wait_ge(S["diag_done"], KI)
        pe.wait_ge(S["w1_loaded"], 16 * 6)
        for t in range(TT):
            turn_in(0, t, S["t3_mm"], S["shift_a"], S["t3_lo"])
        for m in range(KI):
            x_tile(0, m, True)
        wx(0)
        turn_tsb(0)
        for m in range(DG):
            dt_tile(0, m)
        iteration(0, None, 1, True, False)
        iteration(1, 0, 2, False, True)
        with pe.Fori(2, LASTC) as i:
            last_s[0] = (S["mid_lo"], i - 1)
            iteration(i, i - 1, i + 1, False, False)
        last_s[0] = (S["mid_lo"], LASTC - 1)
        iteration(LASTC, LASTC - 1, None, False, False)
        for m in range(DG, KI):
            turn_y(LASTC, m)
        for q in range(4 * TT):
            out_projection(LASTC, q, False)
        for t in range(TT):
            turn_in(LASTC, t, S["t4_mm"], S["shift_b"], S["t4_lo"])
        pe.wait_ge(S["t4_lo"], NCH * TT)
        router(LASTC)
        turn_mid(LASTC)
        for t in range(TT):
            experts(LASTC, t)

    def at_slot(table, s, lag=1):
        return table.get(s - lag, ())


    @block.scalar
    def _(act):
        def exps(i, s, first):
            g, st = s // NS, s % NS
            if not (first and s < 2):
                act.wait_ge(S["scan_done"], i * STEPS + (s - 1))
                r = (s - 2) % STEPS
                nc.scalar.activation(carry[:, r, :], h[:, s % 2, :, CH - 1], ACT.Copy).then_inc(S["carry_done"], 1)
            if st == 0:
                act.wait_ge(S["dt_done"], i * 2 + (g + 1))
            for j in range(DG):
                m = g * DG + j
                ex = nc.scalar.activation(da[:, s % 2, j], dt[:, m], ACT.Exp, scale=a_neg[:, m, st:st + 1])
            ex.then_inc(S["exp_done"], 1)

        def high(n, t, mm, hi, dst):
            act.wait_ge(mm, n * TT + (t + 1))
            nc.scalar.activation(dst[:, :, t * P:(t + 1) * P], ps_s[:].rearrange("p (k q) -> p k q", k=KD), ACT.Copy)\
              .then_inc(hi, 1)

        def x_in(n, m, first):
            act.wait_ge(S["x_mm"], value(n, KI, m))
            if not (first and m < 2):
                act.wait_ge(S["conv_done"], n * (4 * KI) + 4 * (m - 1))
            nc.scalar.activation(xw[:, m % 2, 0:TAPS - 1], hist[:, m], ACT.Copy).then_inc(S["xw_done"], 1)
            nc.scalar.activation(xw[:, m % 2, TAPS - 1:], ps_m[:, m % 2, 0:CH], ACT.Copy, scale=1.0 / WS)\
              .then_inc(S["xw_done"], 1)
            act.wait_ge(S["xw_done"], n * (3 * KI) + (3 * m + 1))
            nc.scalar.activation(hist[:, m], ps_m[:, m % 2, CH - TAPS + 1:CH], ACT.Copy, scale=1.0 / WS)\
              .then_inc(S["xw_done"], 1)

        def x_tanh(n, m):
            act.wait_ge(S["conv_done"], n * (4 * KI) + 4 * (m + 1))
            nc.scalar.activation(th[:, m % 2], cv[:, m % 2], ACT.Tanh).then_inc(S["tanh_done"], 1)

        def u_high(n, m):
            act.wait_ge(S["u_done"], value(n, KI, m))
            nc.scalar.activation(u_h[:, m], u[:, m], ACT.Copy).then_inc(S["u_hi"], 1)

        def gate_tanh(i, m):
            act.wait_ge(S["gate_mm"], value(i, KI, m))
            if m >= 2:
                act.wait_ge(S["gate_sg"], i * KI + (m - 1))
            nc.scalar.activation(th[:, m % 2], ps_m[:, m % 2, 0:CH], ACT.Tanh, scale=0.5 / WS).then_inc(S["gate_th"], 1)

        def dt_abs(n, m):
            act.wait_ge(S["dt_mm"], value(n, KI, m))
            if m == DG:
                act.wait_ge(S["dt_done"], n * 2 + 1)
            nc.scalar.activation(ab[:, m % DG], ps_m[:, m % 2, 0:CH], ACT.Abs, bias=b_dt[:, m:m + 1]).then_inc(S["dt_abs"], 1)

        def dt_log(n, g):
            act.wait_ge(S["dt_abs"], n * KI + (g + 1) * DG)
            nc.scalar.activation(ab[:], ab[:], ACT.Exp, scale=-1.0).then_inc(S["dt_exp"], 1)
            act.wait_ge(S["dt_exp"], n * 2 + (g + 1))
            nc.scalar.activation(ab[:], ab[:], ACT.Ln, bias=1.0).then_inc(S["dt_ln"], 1)

        def ssm_in(n):
            act.wait_ge(S["wx_mm"], n + 1)
            nc.scalar.activation(ssm[:].rearrange("p t w -> p (t w)"), ps_s[:, 0:TT * 64], ACT.Copy, scale=1.0 / WS)\
              .then_inc(S["ssm_done"], 1)

        def tsb_in(n):
            act.wait_ge(S["tsb_mm"], n + 1)
            nc.scalar.activation(tsb[:], ps_s[0:RDT + NS, 0:CH], ACT.Copy).then_inc(S["tsb_done"], 1)

        def y_high(i, m):
            act.wait_ge(S["y_done"], value(i, KI, m))
            nc.scalar.activation(y_h[:, m], y32[:, m % 2], ACT.Copy).then_inc(S["y_hi"], 1)

        def router_in(p):
            act.wait_ge(S["ra_mm"], p + 1)
            nc.scalar.activation(rl[:].rearrange("p t w -> p (t w)"), ps_s[:, 0:TT * RA], ACT.Copy, scale=1.0 / WS)\
              .then_inc(S["rl_done"], 1)

        def router_exp(p):
            act.wait_ge(S["gap_done"], p + 1)
            nc.scalar.activation(e2[:], gap[:], ACT.Exp).then_inc(S["e2_done"], 1)

        def mid_high(p):
            act.wait_ge(S["mid_mm"], p + 1)
            nc.scalar.activation(mid_h[:].rearrange("p t w -> p (t w)"), ps_s[:, 0:TT * P], ACT.Copy).then_inc(S["mid_hi"], 1)

        def iteration(i, p, n, first):
            for s in range(STEPS):
                exps(i, s, first)
                for m in at_slot(DTB_AT, s):
                    dt_abs(i, m)
                if s == 3:
                    dt_log(i, 1)
                if p is not None:
                    for m in at_slot(YB_AT, s):
                        y_high(p, m)
                for m in at_slot(GATE_AT, s):
                    gate_tanh(i, m)
                if n is not None:
                    for t in at_slot(T3_AT, s):
                        high(n, t, S["t3_mm"], S["t3_hi"], h3_h)
                    for m in at_slot(XT_AT, s):
                        x_in(n, m, False)
                    for m in at_slot(XT_AT, s, 2):
                        x_tanh(n, m)
                    for m in at_slot(XT_AT, s, 3):
                        u_high(n, m)
                for m in at_slot(YA_AT, s):
                    y_high(i, m)
                if n is not None and s == WX_AT + 1:
                    ssm_in(n)
                if p is not None:
                    for t in at_slot(T4_AT, s):
                        high(p, t, S["t4_mm"], S["t4_hi"], h4_h)
                if n is not None and s == TSB_AT + 1:
                    tsb_in(n)
                if p is not None and s == RA_AT + 1:
                    router_in(p)
                if n is not None:
                    for m in at_slot(DTA_AT, s):
                        dt_abs(n, m)
                    if s == 27:
                        dt_log(n, 0)
                if p is not None and s == RA_AT + 2:
                    router_exp(p)
                if p is not None and s == MID_AT + 1:
                    mid_high(p)

        act.wait_ge(S["w1_loaded"], 16 * 6)
        nc.scalar.activation(a_exp[:], a_log[:], ACT.Exp).then_inc(S["aexp_done"], 1)
        act.wait_ge(S["aneg_done"], 1)
        act.wait_ge(S["zeros_done"], 2)
        for t in range(TT):
            high(0, t, S["t3_mm"], S["t3_hi"], h3_h)
        for m in range(KI):
            x_in(0, m, True)
            x_tanh(0, m)
            u_high(0, m)
        ssm_in(0)
        tsb_in(0)
        for m in range(DG):
            dt_abs(0, m)
        dt_log(0, 0)
        iteration(0, None, 1, True)
        iteration(1, 0, 2, False)
        with act.Fori(2, LASTC) as i:
            iteration(i, i - 1, i + 1, False)
        iteration(LASTC, LASTC - 1, None, False)
        for m in range(DG, KI):
            y_high(LASTC, m)
        for t in range(TT):
            high(LASTC, t, S["t4_mm"], S["t4_hi"], h4_h)
        router_in(LASTC)
        router_exp(LASTC)
        mid_high(LASTC)

    @block.gpsimd
    def _(pool):
        def db(i, s, first):
            g, st = s // NS, s % NS
            if st % BQ == 0 and g == 0:
                pool.wait_ge(b_in[st // BQ], i * 16 + 16)
            if st == 0:
                pool.wait_ge(S["dtu_done"], i * 2 + (g + 1))
            if not (first and s < 2):
                pool.wait_ge(S["scan_done"], i * STEPS + (s - 1))
            nc.gpsimd.tensor_tensor(dbu[:, s % 2], dtu[:, g * DG:(g + 1) * DG],
                                    b_all[:, st, :].unsqueeze(1).to_broadcast([P, DG, CH]), ALU.mult).then_inc(S["dbu_done"], 1)

        def inv_std(n, aggr, ve, rs):
            pool.wait_ge(aggr, n * TT + TT)
            pool.sem_inc(S["met_pool"], 1)
            nc.gpsimd.tensor_scalar(veps[:], mv[:, :, 1], LN_EPS, None, ALU.add).then_inc(ve, 1)
            pool.wait_ge(ve, n + 1)
            nc.gpsimd.tensor_tensor(rstd[:], veps[:], W["mhalf"][:, 0:TT], ALU.pow).then_inc(rs, 1)

        def modulate(n, q, norm, scale, shift):
            pool.wait_ge(norm, n * TT + TT)
            nc.gpsimd.tensor_tensor(xa[:], xa[:], mod[:, q + 1, :].unsqueeze(1).to_broadcast([P, TT, D]), ALU.mult)\
              .then_inc(scale, 1)
            pool.wait_ge(scale, n + 1)
            nc.gpsimd.tensor_tensor(xa[:], xa[:], mod[:, q, :].unsqueeze(1).to_broadcast([P, TT, D]), ALU.add)\
              .then_inc(shift, 1)

        def u_low(n, m):
            pool.wait_ge(S["u_hi"], value(n, KI, m))
            nc.gpsimd.tensor_tensor(u_l[:, m], u[:, m], u_h[:, m], ALU.subtract).then_inc(S["u_lo"], 1)

        def y_low(i, m):
            pool.wait_ge(S["y_hi"], value(i, KI, m))
            nc.gpsimd.tensor_tensor(y_l[:, m], y32[:, m % 2], y_h[:, m], ALU.subtract).then_inc(S["y_lo"], 1)

        def rms_pow(n):
            pool.wait_ge(S["me_done"], n * 2 + 2)
            nc.gpsimd.tensor_tensor(rms[:].rearrange("p t w -> p (t w)"), mse[:].rearrange("p t w -> p (t w)"),
                                    W["mhalf"][:, 0:TT * 3], ALU.pow).then_inc(S["rms_done"], 1)

        def dt_u(n, g):
            pool.wait_ge(S["dt_done"], n * 2 + (g + 1))
            grp = slice(g * DG, (g + 1) * DG)
            nc.gpsimd.tensor_tensor(dtu[:, grp], dt[:, grp], u[:, grp], ALU.mult).then_inc(S["dtu_done"], 1)

        def iteration(i, p, n, first):
            for s in range(STEPS):
                db(i, s, first)
                if p is not None:
                    for m in at_slot(YB_AT, s):
                        y_low(p, m)
                if n is not None and s == 2:
                    inv_std(n, S["aggr_a"], S["veps_a"], S["rstd_a"])
                if s == 3:
                    if n is not None:
                        modulate(n, 0, S["norm_a"], S["scale_a"], S["shift_a"])
                    dt_u(i, 1)
                if n is not None:
                    for m in at_slot(XT_AT, s, 3):
                        u_low(n, m)
                for m in at_slot(YA_AT, s):
                    y_low(i, m)
                if p is not None and s == 17:
                    inv_std(p, S["aggr_b"], S["veps_b"], S["rstd_b"])
                if p is not None and s == 18:
                    modulate(p, 2, S["norm_b"], S["scale_b"], S["shift_b"])
                if n is not None and s == 21:
                    rms_pow(n)
                if n is not None and s == 27:
                    dt_u(n, 0)

        pool.wait_ge(S["mod_loaded"], 16 * 4)
        inv_std(0, S["aggr_a"], S["veps_a"], S["rstd_a"])
        modulate(0, 0, S["norm_a"], S["scale_a"], S["shift_a"])
        for m in range(KI):
            u_low(0, m)
        rms_pow(0)
        dt_u(0, 0)
        iteration(0, None, 1, True)
        iteration(1, 0, 2, False)
        with pool.Fori(2, LASTC) as i:
            iteration(i, i - 1, i + 1, False)
        iteration(LASTC, LASTC - 1, None, False)
        for m in range(DG, KI):
            y_low(LASTC, m)
        inv_std(LASTC, S["aggr_b"], S["veps_b"], S["rstd_b"])
        modulate(LASTC, 2, S["norm_b"], S["scale_b"], S["shift_b"])

    @block.vector
    def _(dve):
        def scans(i, s, first):
            dve.wait_ge(S["exp_done"], value(i, STEPS, s))
            dve.wait_ge(S["dbu_done"], value(i, STEPS, s))
            for j in range(DG):
                sc = nc.vector.tensor_tensor_scan(h[:, s % 2, j], da[:, s % 2, j], dbu[:, s % 2, j],
                                                  carry[:, s, j:j + 1], ALU.mult, ALU.add)
            sc.then_inc(S["scan_done"], 1)

        def add_state(i, s):
            g, st, use = s // NS, s % NS, use_of_step(s)
            dve.wait_ge(S["hT_done"], value(i, USES, use))
            dve.wait_ge(S["hT_used"], i * USES + use)
            for t in range(TT):
                part = acc[:, t, g * DG * P:(g + 1) * DG * P]
                st_ = nc.vector.scalar_tensor_tensor(part, ps_h[:, use % 2, t], c_cur[:, t, st:st + 1], part,
                                                     ALU.mult, ALU.add)
            st_.then_inc(S["hT_used"], 1)

        def start_acc(i, g, first):
            use = 0 if g == 0 else UB_AT + 1
            dve.wait_ge(S["hT_done"], value(i, USES, use))
            if not first:
                dve.wait_ge(S["y_mm"], (i - 1) * KI + (g + 1) * DG)
            for t in range(TT):
                cp = nc.vector.tensor_copy(acc[:, t, g * DG * P:(g + 1) * DG * P], ps_h[:, use % 2, t])
            cp.then_inc(S["hT_used"], 1)

        def keep_c(i, first):
            if not first:
                dve.wait_ge(S["hT_used"], i * USES)
            nc.vector.tensor_copy(c_cur[:], ssn[:, :, RDT + NS:]).then_inc(S["c_done"], 1)
            dve.wait_ge(S["c_done"], i + 1)

        def statistics(n, src, st, ag):
            for t in range(TT):
                nc.vector.bn_stats(stats[:, t], src[:, t]).then_inc(st, 1)
            for t in range(TT):
                dve.wait_ge(st, n * TT + (t + 1))
                dve.sem_inc(S["met_dve"], 1)
                nc.vector.bn_aggr(mv[:, t], stats[:, t]).then_inc(ag, 1)

        def normalise(n, src, rs, norm):
            dve.wait_ge(rs, n + 1)
            for t in range(TT):
                nc.vector.tensor_scalar(xa[:, t], src[:, t], mv[:, t, 0:1], rstd[:, t:t + 1], ALU.subtract, ALU.mult)\
                  .then_inc(norm, 1)

        def low(n, t, hi, lo, src, dst):
            dve.wait_ge(hi, n * TT + (t + 1))
            tok = slice(t * P, (t + 1) * P)
            nc.vector.tensor_tensor(dst[:, :, tok], ps_s[:].rearrange("p (k q) -> p k q", k=KD), src[:, :, tok],
                                    ALU.subtract).then_inc(lo, 1)

        def conv(n, m, first):
            base = n * (4 * KI) + 4 * m
            dve.wait_ge(S["xw_done"], n * (3 * KI) + 3 * (m + 1))
            if not (first and m < 2):
                dve.wait_ge(S["u_done"], n * KI + (m - 1))
            for a, tap in enumerate(range(TAPS - 1, -1, -1)):
                w = taps[:, m, tap:tap + 1]
                src = xw[:, m % 2, tap:tap + CH]
                if a == 0:
                    op = nc.vector.tensor_scalar(cv[:, m % 2], src, w, taps[:, m, TAPS:TAPS + 1], ALU.mult, ALU.add)
                else:
                    dve.wait_ge(S["conv_done"], n * (4 * KI) + (4 * m + a))
                    op = nc.vector.scalar_tensor_tensor(cv[:, m % 2], src, w, cv[:, m % 2], ALU.mult, ALU.add)
                op.then_inc(S["conv_done"], 1)

        def make_u(n, m):
            dve.wait_ge(S["tanh_done"], value(n, KI, m))
            nc.vector.scalar_tensor_tensor(u[:, m], th[:, m % 2], 1.0, cv[:, m % 2], ALU.add, ALU.mult).then_inc(S["u_done"], 1)

        def make_sg(i, m):
            dve.wait_ge(S["gate_th"], value(i, KI, m))
            nc.vector.scalar_tensor_tensor(sg[:, m], th[:, m % 2], 1.0, ps_m[:, m % 2, 0:CH], ALU.add, ALU.mult)\
              .then_inc(S["gate_sg"], 1)

        def dt_max(n, m):
            dve.wait_ge(S["dt_abs"], value(n, KI, m))
            nc.vector.tensor_scalar(dt[:, m], ps_m[:, m % 2, 0:CH], b_dt[:, m:m + 1], 0.0, ALU.add, ALU.max)\
              .then_inc(S["dt_max"], 1)

        def dt_add(n, g):
            dve.wait_ge(S["dt_ln"], n * 2 + (g + 1))
            dve.wait_ge(S["dt_max"], n * KI + (g + 1) * DG)
            grp = slice(g * DG, (g + 1) * DG)
            nc.vector.tensor_tensor(dt[:, grp], dt[:, grp], ab[:], ALU.add).then_inc(S["dt_done"], 1)

        def mean_squares(n):
            dve.wait_ge(S["ssm_done"], n + 1)
            nc.vector.tensor_tensor(ssq[:], ssm[:], ssm[:], ALU.mult).then_inc(S["sq_done"], 1)
            dve.wait_ge(S["sq_done"], n + 1)
            nc.vector.tensor_reduce(msq[:, :, 0:1], ssq[:, :, 0:RDT].unsqueeze(2), X, ALU.add).then_inc(S["ms_done"], 1)
            nc.vector.tensor_reduce(msq[:, :, 1:3], ssq[:, :, RDT:].rearrange("p t (b s) -> p t b s", b=2), X, ALU.add)\
              .then_inc(S["ms_done"], 1)
            dve.wait_ge(S["ms_done"], n * 2 + 2)
            nc.vector.tensor_scalar(mse[:, :, 0:1], msq[:, :, 0:1], 1.0 / RDT, RMS_EPS, ALU.mult, ALU.add).then_inc(S["me_done"], 1)
            nc.vector.tensor_scalar(mse[:, :, 1:3], msq[:, :, 1:3], 1.0 / NS, RMS_EPS, ALU.mult, ALU.add).then_inc(S["me_done"], 1)

        def rms_apply(n):
            dve.wait_ge(S["rms_done"], n + 1)
            nc.vector.tensor_tensor(ssn[:, :, 0:RDT], ssm[:, :, 0:RDT], rms[:, :, 0:1].to_broadcast([P, TT, RDT]), ALU.mult)\
              .then_inc(S["ssn_done"], 1)
            nc.vector.tensor_tensor(ssn[:, :, RDT:].rearrange("p t (b s) -> p t b s", b=2),
                                    ssm[:, :, RDT:].rearrange("p t (b s) -> p t b s", b=2),
                                    rms[:, :, 1:3].unsqueeze(3).to_broadcast([P, TT, 2, NS]), ALU.mult).then_inc(S["ssn_done"], 1)

        def make_y(i, m, first):
            dve.wait_ge(S["y_mm"], value(i, KI, m))
            if not (first and m < 2):
                dve.wait_ge(S["y_lo"], i * KI + (m - 1))
            nc.vector.scalar_tensor_tensor(y32[:, m % 2], ps_s[:, 0:CH], 0.5 / WS, sg[:, m], ALU.mult, ALU.mult)\
              .then_inc(S["y_done"], 1)

        def add_out_projection(p, t):
            dve.wait_ge(S["wo_mm"], value(p, TT, t))
            dve.wait_ge(S["x3_loaded"], p * 16 + 16)
            nc.vector.scalar_tensor_tensor(x3[:, t], ps_o[:], 1.0 / WS, x3[:, t], ALU.mult, ALU.add).then_inc(S["x3_done"], 1)

        def choose(p):
            dve.wait_ge(S["rl_done"], p + 1)
            dve.sem_inc(S["met_dve"], 1)
            for t in range(TT):
                nc.vector.max(top[:, t], rl[:, t, 0:NE]).then_inc(S["top_done"], 1)
            for t in range(TT):
                dve.wait_ge(S["top_done"], p * TT + (t + 1))
                dve.sem_inc(S["met_dve"], 1)
                nc.vector.max_index(top_at[:, t], top[:, t], rl[:, t, 0:NE]).then_inc(S["top_at_done"], 1)
            nc.vector.tensor_tensor(gap[:], top[:, :, 1], top[:, :, 0], ALU.subtract).then_inc(S["gap_done"], 1)
            dve.wait_ge(S["top_at_done"], p * TT + TT)
            nc.vector.tensor_copy(at[:], top_at[:, :, 0:2]).then_inc(S["at_done"], 1)

        def weigh(p):
            dve.wait_ge(S["e2_done"], p + 1)
            nc.vector.tensor_scalar(e2p[:], e2[:], 1.0, None, ALU.add).then_inc(S["e2p_done"], 1)
            dve.wait_ge(S["e2p_done"], p + 1)
            nc.vector.reciprocal(inv[:], e2p[:]).then_inc(S["inv_done"], 1)
            dve.wait_ge(S["inv_done"], p + 1)
            nc.vector.tensor_scalar(w12[:, :, 0], inv[:], 2.0, None, ALU.mult).then_inc(S["w1_done"], 1)
            dve.wait_ge(S["w1_done"], p + 1)
            nc.vector.tensor_tensor(w12[:, :, 1], w12[:, :, 0], e2[:], ALU.mult).then_inc(S["w2_done"], 1)
            dve.wait_ge(S["w2_done"], p + 1)
            dve.wait_ge(S["at_done"], p + 1)
            for t in range(TT):
                for b in range(2):
                    nc.vector.tensor_scalar(wd[:, b, t], expert[:], at[:, t, b:b + 1], w12[:, t, b:b + 1],
                                            ALU.is_equal, ALU.mult).then_inc(S["m1_done"], 1)
            dve.wait_ge(S["m1_done"], p * (2 * TT) + 2 * TT)
            nc.vector.tensor_tensor(wd[:, 0], wd[:, 0], wd[:, 1], ALU.add).then_inc(S["wd_done"], 1)
            dve.wait_ge(S["wd_done"], p + 1)
            nc.vector.tensor_tensor(mid[:].rearrange("p t (e r) -> p t e r", e=NE),
                                    rl[:, :, NE:].rearrange("p t (e r) -> p t e r", e=NE),
                                    wd[:, 0].unsqueeze(3).to_broadcast([P, TT, NE, LORA]), ALU.mult).then_inc(S["mid_done"], 1)

        def mid_low(p):
            dve.wait_ge(S["mid_hi"], p + 1)
            nc.vector.tensor_tensor(mid_l[:].rearrange("p t w -> p (t w)"), ps_s[:, 0:TT * P],
                                    mid_h[:].rearrange("p t w -> p (t w)"), ALU.subtract).then_inc(S["mid_lo"], 1)

        def add_experts(p, t):
            dve.wait_ge(S["base_mm"], value(p, TT, t))
            nc.vector.scalar_tensor_tensor(x3[:, t], ps_o[:], 1.0 / WS, x3[:, t], ALU.mult, ALU.add).then_inc(S["out_done"], 1)

        def iteration(i, p, n, first, second):
            for s in range(STEPS):
                scans(i, s, first)
                if s == 0 and not first:
                    add_state(i - 1, STEPS - 1)
                if s == 0:
                    keep_c(i, first)
                if s == 1:
                    start_acc(i, 0, first)
                if s == UB_AT + 1:
                    start_acc(i, 1, first)
                if s:
                    add_state(i, s - 1)
                for m in at_slot(DTB_AT, s):
                    dt_max(i, m)
                if s == 3:
                    dt_add(i, 1)
                if p is not None:
                    for m in at_slot(YB_AT, s):
                        make_y(p, m, False)
                if n is not None and s == 2:
                    dve.wait_ge(S["xa_loaded"], n * 16 + 16)
                    statistics(n, xa, S["stats_a"], S["aggr_a"])
                if n is not None and s == 3:
                    normalise(n, xa, S["rstd_a"], S["norm_a"])
                for m in at_slot(GATE_AT, s):
                    make_sg(i, m)
                if n is not None:
                    for t in at_slot(T3_AT, s):
                        low(n, t, S["t3_hi"], S["t3_lo"], h3_h, h3_l)
                    for m in at_slot(XT_AT, s):
                        conv(n, m, False)
                    for m in at_slot(XT_AT, s, 2):
                        make_u(n, m)
                if p is not None and s == 12:
                    add_out_projection(p, 0)
                if p is not None and s == 16:
                    add_out_projection(p, 1)
                    dve.wait_ge(S["x3_done"], p * TT + TT)
                    statistics(p, x3, S["stats_b"], S["aggr_b"])
                if p is not None and s == 17:
                    normalise(p, x3, S["rstd_b"], S["norm_b"])
                for m in at_slot(YA_AT, s):
                    make_y(i, m, first)
                if n is not None and s == WX_AT + 1:
                    mean_squares(n)
                if n is not None and s == WX_AT + 2:
                    rms_apply(n)
                if p is not None:
                    for t in at_slot(T4_AT, s):
                        low(p, t, S["t4_hi"], S["t4_lo"], h4_h, h4_l)
                if n is not None:
                    for m in at_slot(DTA_AT, s):
                        dt_max(n, m)
                if p is not None and s == RA_AT + 1:
                    choose(p)
                if p is not None and s == RA_AT + 2:
                    weigh(p)
                if n is not None and s == 27:
                    dt_add(n, 0)
                if p is not None and s == MID_AT + 1:
                    mid_low(p)
                if p is not None:
                    for t in at_slot(BASE_AT, s):
                        add_experts(p, t)

        nc.vector.memset(hist[:], 0.0).then_inc(S["zeros_done"], 1)
        nc.vector.memset(carry[:], 0.0).then_inc(S["zeros_done"], 1)
        dve.wait_ge(S["w1_loaded"], 16 * 6)
        nc.vector.tensor_scalar(taps[:], taps_raw[:], 0.5, None, ALU.mult).then_inc(S["taps_done"], 1)
        for m in range(KI):
            nc.vector.tensor_scalar(diag_d[:, m], W["ident"][:], d_vec[:, m:m + 1], None, ALU.mult).then_inc(S["diag_done"], 1)
        dve.wait_ge(S["aexp_done"], 1)
        nc.vector.tensor_scalar(a_neg[:], a_exp[:], -1.0, None, ALU.mult).then_inc(S["aneg_done"], 1)
        dve.wait_ge(S["taps_done"], 1)
        dve.wait_ge(S["zeros_done"], 2)
        dve.wait_ge(S["xa_loaded"], 16)
        statistics(0, xa, S["stats_a"], S["aggr_a"])
        normalise(0, xa, S["rstd_a"], S["norm_a"])
        for t in range(TT):
            low(0, t, S["t3_hi"], S["t3_lo"], h3_h, h3_l)
        for m in range(KI):
            conv(0, m, True)
            make_u(0, m)
        mean_squares(0)
        rms_apply(0)
        for m in range(DG):
            dt_max(0, m)
        dt_add(0, 0)
        iteration(0, None, 1, True, False)
        iteration(1, 0, 2, False, True)
        with dve.Fori(2, LASTC) as i:
            iteration(i, i - 1, i + 1, False, False)
        iteration(LASTC, LASTC - 1, None, False, False)
        add_state(LASTC, STEPS - 1)
        for m in range(DG, KI):
            make_y(LASTC, m, False)
        for t in range(TT):
            add_out_projection(LASTC, t)
        dve.wait_ge(S["x3_done"], NCH * TT)
        statistics(LASTC, x3, S["stats_b"], S["aggr_b"])
        normalise(LASTC, x3, S["rstd_b"], S["norm_b"])
        for t in range(TT):
            low(LASTC, t, S["t4_hi"], S["t4_lo"], h4_h, h4_l)
        choose(LASTC)
        weigh(LASTC)
        mid_low(LASTC)
        for t in range(TT):
            add_experts(LASTC, t)


def kernel(**inputs):
    import numpy as np
    import concourse.bacc as bacc
    from concourse.bass_utils import run_bass_kernel_spmd

    I = {k: np.asarray(v) for k, v in inputs.items()}
    arrays = {
        "x": I["L0_attn_data"].reshape(T, D),
        "mask": I["L0_attn_mask"].T, "w0": I["L0_attn_weight"].T, "bias": I["L0_attn_bias"].reshape(1, D),
        "gate_w": I["L0_ffn_gate_w"].T, "up_w": I["L0_ffn_up_w"].T, "down_w": I["L0_ffn_down_w"].T,
        "gate_a": I["L0_ffn_gate_a"], "gate_b": I["L0_ffn_gate_b"].T,
        "up_a": I["L0_ffn_up_a"], "up_b": I["L0_ffn_up_b"].T,
        "down_a": I["L0_ffn_down_a"], "down_b": I["L0_ffn_down_b"].T,
        "c": np.stack([I["L0_c"].reshape(KD, P), I["L1_c"].reshape(KD, P)]).transpose(2, 0, 1),
        "wmod0": I["L0_wmod"], "wmod1": I["L1_wmod"],
        "W_in": I["L1_attn_W_in"].T,
        "conv": np.concatenate([I["L1_attn_conv_w"], I["L1_attn_conv_b"].reshape(DI, 1)], axis=1)
        .reshape(KI, P, TAPS + 1).transpose(1, 0, 2),
        "W_x": I["L1_attn_W_x"].T, "W_dt": I["L1_attn_W_dt"].T,
        "b_dt": I["L1_attn_b_dt"].reshape(KI, P).T,
        "A_log": I["L1_attn_A_log"].reshape(KI, P, NS).transpose(1, 0, 2),
        "D": I["L1_attn_D"].reshape(KI, P).T,
        "W_out": I["L1_attn_W_out"].T, "base_W": I["L1_ffn_base_W"].T,
        "router_A": np.concatenate([I["L1_ffn_router_W"].T, I["L1_ffn_lora_A"].transpose(1, 0, 2).reshape(D, ER)], axis=1),
        "lora_B": I["L1_ffn_lora_B"].reshape(ER, D),
        "ident": np.eye(P, dtype=np.float32),
        "blk32": np.kron(np.eye(P // 32, dtype=np.float32), np.ones((32, 32), np.float32)),
        "expert": np.tile(np.arange(NE, dtype=np.float32), (P, 1)),
    }
    nc = bacc.Bacc("TRN2", target_bir_lowering=False, num_devices=1)
    A, feed = {}, {}
    for name, a in arrays.items():
        a = np.ascontiguousarray(a)
        feed[f"in_{name}"] = a
        A[name] = nc.dram_tensor(f"in_{name}", a.shape, mybir.dt.from_np(a.dtype), kind="ExternalInput").ap()
    for name in ("mask", "w0", "W_out", "base_W", "W_x", "router_A"):
        A[name] = A[name].rearrange("(k p) n -> p k n", p=P)
    for name in ("gate_w", "up_w", "W_in"):
        A[name] = A[name].rearrange("(k p) n -> k p n", p=P)
    out = nc.dram_tensor("out", (1, T, D), F32, kind="ExternalOutput").ap()
    build(nc, A, out)
    r = run_bass_kernel_spmd(nc, [feed], core_ids=[0])
    return r.results[0]["out"]
```

```python
from contextlib import ExitStack

from concourse import mybir

F32 = mybir.dt.float32
F16 = mybir.dt.float16
I32 = mybir.dt.int32
U32 = mybir.dt.uint32
ALU = mybir.AluOpType
ACT = mybir.ActivationFunctionType
X = mybir.AxisListType.X

P = 128
T = 2048
D = 512
KD = D // P
HID = 1376
KH = -(-HID // P)
LORA = 16
NB = D // 32
CH = 256
TT = CH // P
NCH = T // CH
DI = 1024
KI = DI // P
NS = 16
RDT = 32
TAPS = 4
NE = 8
ER = NE * LORA
RA = NE + ER
WS = 64.0
DG = 4
NDG = KI // DG
AHEAD = 4
STEPS = NDG * NS
LN_EPS = 1e-5
RMS_EPS = 1e-6

DTB_AT = {0: (4, 5), 1: (6, 7)}
YB_AT = {1: (4,), 2: (5,), 3: (6,), 4: (7,)}
GB_AT = {2: (4,), 3: (5, 6), 4: (7,)}
T3_AT = {4: (0,), 5: (1,)}
UB_AT = 6
XT_AT = {7 + m: (m,) for m in range(KI)}
WO_AT = {0: (0,), 1: (1,), 6: (2,), 7: (3,), 9: (4,), 11: (5,), 13: (6,), 15: (7,)}
YA_AT = {17: (0,), 18: (1,), 19: (2,), 20: (3,)}
WX_AT = 20
T4_AT = {20: (0,), 21: (1,)}
GA_AT = {22: (0,), 23: (1,), 27: (2,), 28: (3,)}
RA_AT = 23
TSB_AT = 24
DTA_AT = {25: (0, 1), 26: (2, 3)}
MID_AT = 26
BASE_AT = {24: (0,), 28: (1,), 29: (2,), 30: (3,)}

def hid_rows(m):
    return min(P, HID - m * P)


def value(k, per, j):
    return k * per + (j + 1)


def build(nc, A, out):
    with ExitStack() as ctx:
        def sb(name, shape, dt=F32, c=ctx):
            return c.enter_context(nc.sbuf_tensor(name, shape, dt))

        def ps(name, shape, c):
            return c.enter_context(nc.psum_tensor(name, shape, F32))

        def sems(names, c=ctx):
            return {n: c.enter_context(nc.semaphore(n)) for n in names.split()}

        x2_dram = nc.dram_tensor("x2_scratch", (T, D), F32, kind="Internal").ap()
        bt_dram = nc.dram_tensor("bt_scratch", (NCH, 1, NS * CH), F32, kind="Internal").ap()

        wi_h = sb("wi_h", [P, KD, 2 * DI], F16)
        wi_l = sb("wi_l", [P, KD, 2 * DI], F16)
        wo_h = sb("wo_h", [P, KI, D], F16)
        wo_l = sb("wo_l", [P, KI, D], F16)
        ba_h = sb("ba_h", [P, KD, D], F16)
        ba_l = sb("ba_l", [P, KD, D], F16)
        lb_h = sb("lb_h", [P, D], F16)
        lb_l = sb("lb_l", [P, D], F16)
        wx_h = sb("wx_h", [P, KI, RDT + 2 * NS], F16)
        wx_l = sb("wx_l", [P, KI, RDT + 2 * NS], F16)
        ra_h = sb("ra_h", [P, KD, RA], F16)
        ra_l = sb("ra_l", [P, KD, RA], F16)
        ident = sb("ident", [P, P])
        mhalf = sb("mhalf", [P, 8])
        epsilon = sb("epsilon", [P, TT])
        ones = sb("ones", [1, P], F16)
        b_in = sb("b_in", [P, 2 * KI])
        bb_h = sb("bb_h", [1, D], F16)
        bb_l = sb("bb_l", [1, D], F16)
        rb_h = sb("rb_h", [1, RA], F16)
        rb_l = sb("rb_l", [1, RA], F16)
        W = {"wi_h": wi_h, "wi_l": wi_l, "wo_h": wo_h, "wo_l": wo_l, "ba_h": ba_h, "ba_l": ba_l, "lb_h": lb_h, "lb_l": lb_l,
             "wx_h": wx_h, "wx_l": wx_l, "ra_h": ra_h, "ra_l": ra_l, "ident": ident, "mhalf": mhalf,
             "epsilon": epsilon, "ones": ones, "b_in": b_in, "bb_h": bb_h, "bb_l": bb_l, "rb_h": rb_h, "rb_l": rb_l}
        W.update(sems("const_loaded mhalf_set bias_done"))

        with ExitStack() as layer0:
            w0_h = sb("w0_h", [P, KD, D], F16, layer0)
            w0_l = sb("w0_l", [P, KD, D], F16, layer0)
            g_h = sb("g_h", [P, KD, HID], F16, layer0)
            g_l = sb("g_l", [P, KD, HID], F16, layer0)
            u_h = sb("u_h", [P, KD, HID], F16, layer0)
            u_l = sb("u_l", [P, KD, HID], F16, layer0)
            d_h = sb("d_h", [P, KH, D], F16, layer0)
            d_l = sb("d_l", [P, KH, D], F16, layer0)
            mod0 = sb("mod0", [P, 2, D], F32, layer0)
            scale0 = sb("scale0", [P, 2, KD], F32, layer0)
            shift0 = sb("shift0", [P, 2, KD], F32, layer0)
            ga_bias = sb("ga_bias", [P, D], F32, layer0)

            W0 = {"w0_h": w0_h, "w0_l": w0_l, "g_h": g_h, "g_l": g_l, "u_h": u_h, "u_l": u_l, "d_h": d_h, "d_l": d_l,
                  "mod0": mod0, "scale0": scale0, "shift0": shift0, "ga_bias": ga_bias}
            W0.update(W)
            with ExitStack() as c:
                setup(nc, A, W0, c, sb, ps, sems)
            with ExitStack() as c:
                layer_0(nc, A, x2_dram, W0, c, sb, ps, sems)
        with ExitStack() as c:
            layer_1(nc, A, x2_dram, bt_dram, out, W, c, sb, ps, sems)


def setup(nc, A, W, c, sb, ps, sems):
    SLOTS = 3
    stage = sb("stage", [P, SLOTS, 2048], F32, c)
    wmod = sb("wmod", [P, 2, KD, D], F32, c)
    lora_f = sb("lora_f", [80, 2, HID], F32, c)
    lora_s = sb("lora_s", [80, 2, 2, HID], F16, c)
    cvec = sb("cvec", [P, 2, KD], F32, c)
    silu_c = sb("silu_c", [P, 2, KD], F32, c)
    silu_cb = sb("silu_cb", [P, 2, KD, P], F32, c)
    blk32 = sb("blk32", [P, P], F32, c)
    msum = sb("msum", [P, KD * NB], F32, c)
    mon = sb("mon", [P, KD * NB], F32, c)
    gate1 = sb("gate1", [P, 2, D], F32, c)
    scale = sb("scale", [P, 2, KD], F32, c)
    shift = sb("shift", [P, 2, KD], F32, c)
    shift_b = sb("shift_b", [P, 2, KD, P], F32, c)
    sgn = sb("sgn", [P, D], F32, c)
    picked = sgn[:].rearrange("p (m q) -> p m q", q=P)
    ps_lora = ps("ps_lora", [P, 2048], c)
    ps_mod = ps("ps_mod", [P, 2, D], c)
    ps_mask = ps("ps_mask", [P, D], c)
    ps_row = ps("ps_row", [P, D], c)
    S = sems("cvec_loaded silu_c_done silu_cb_done wmod_0 wmod_1 wmod_used mod_step mod_done "
             "stage_0 stage_1 stage_2 stage_pre stage_hi stage_lo lora_loaded lora_zero lora_hi lora_split lora_mm blk_loaded bias_mm "
             "mask_sums mask_mm bias_loaded row_step", c)
    wmod_in = (S["wmod_0"], S["wmod_1"])
    stage_in = (S["stage_0"], S["stage_1"], S["stage_2"])

    pieces = []

    def piece(kind, no, src, rows, high, low, parts, ln=None):
        width = high.shape[-1]
        cuts = []
        for k in range(parts):
            hi_k, lo_k = (high[:, k], low[:, k]) if len(high.shape) == 3 else (high, low)
            col = None if ln is None else scale[0:rows, ln, (k if parts > 1 else no):(k if parts > 1 else no) + 1]
            cuts.append((k * width, (k + 1) * width, hi_k, lo_k, col))
        if ln is None and len(high.shape) == 3:
            cuts = [(0, parts * width, high.rearrange("p k n -> p (k n)"), low.rearrange("p k n -> p (k n)"), None)]
        pieces.append((kind, no, parts * width, rows, src, cuts))

    pieces.append(("mask", 0, KD * D, P, A["mask"], []))
    piece("w0", 0, A["w0"], P, W["w0_h"][:], W["w0_l"][:], KD)
    for k in range(KD):
        piece("gate", k, A["gate_w"][k], P, W["g_h"][:, k], W["g_l"][:, k], 1)
    for k in range(KD):
        piece("up", k, A["up_w"][k], P, W["u_h"][:, k], W["u_l"][:, k], 1)
    for a, b in ((0, 4), (4, 8), (8, 10)):
        piece("down", a, A["down_w"][0:10 * P, :].rearrange("(k p) n -> p k n", p=P)[:, a:b], P,
              W["d_h"][:, a:b], W["d_l"][:, a:b], b - a)
    piece("down", 10, A["down_w"][10 * P:HID, :], HID - 10 * P, W["d_h"][0:HID - 10 * P, 10], W["d_l"][0:HID - 10 * P, 10], 1)
    for k in range(KD):
        piece("win", k, A["W_in"][k], P, W["wi_h"][:, k], W["wi_l"][:, k], 1, 0)
    for a in range(2):
        piece("wout", a, A["W_out"][:, 4 * a:4 * a + 4], P, W["wo_h"][:, 4 * a:4 * a + 4], W["wo_l"][:, 4 * a:4 * a + 4], 4)
    piece("base", 0, A["base_W"], P, W["ba_h"][:], W["ba_l"][:], KD, 1)
    piece("ra", 0, A["router_A"], P, W["ra_h"][:], W["ra_l"][:], KD, 1)
    piece("lb", 0, A["lora_B"], P, W["lb_h"][:], W["lb_l"][:], 1)
    piece("wx", 0, A["W_x"], P, W["wx_h"][:], W["wx_l"][:], KI)
    N = len(pieces)
    kinds = [x[0] for x in pieces]
    before = {3: ((0, 0),), 4: ((0, 1),), 5: ((0, 3),), 6: ((0, 4),), 7: ((0, 2),), 8: ((0, 5),), 9: ((1, 0),), 11: ((1, 1),),
              13: ((1, 2),), 15: ((1, 3),), 16: ((1, 4),), 17: ((1, 5),)}
    mods = [m for n in range(N) for m in before.get(n, ())]
    mod_no = {m: i for i, m in enumerate(mods)}
    PRE = ("w0", "gate", "up", "down", "wout", "base", "lb")
    pre_no = {n: i + 1 for i, n in enumerate(n for n in range(N) if kinds[n] in PRE)}
    BIAS = ("win", "base", "ra")
    bias_no = {n: i + 1 for i, n in enumerate(n for n in range(N) if kinds[n] in BIAS)}
    loras = [n for n in range(N) if kinds[n] in ("gate", "up", "down")]
    lora_no = {n: i + 1 for i, n in enumerate(loras)}
    last_win = max(n for n in range(N) if kinds[n] == "win")
    lora_widths = ((D, HID), (D, HID), (HID, D))
    block = c.enter_context(nc.Block())

    @block.sync
    def _(sp):
        sp.dma_start(cvec[:], A["c"]).then_inc(S["cvec_loaded"], 16)
        sp.dma_start(blk32[:], A["blk32"]).then_inc(S["blk_loaded"], 16)

        def load_lora(r):
            name = ("gate", "up", "down")[r]
            wa, wb = lora_widths[r]
            if r == 0:
                sp.wait_ge(S["lora_zero"], 1)
            else:
                sp.wait_ge(S["lora_split"], 2 * r)
                sp.wait_ge(S["lora_hi"], 2 * r)
            for at in (0, 32, 64):
                sp.dma_start(lora_f[at:at + LORA, 0, 0:wa], A[name + "_a"]).then_inc(S["lora_loaded"], 16)
                sp.dma_start(lora_f[at:at + LORA, 1, 0:wb], A[name + "_b"]).then_inc(S["lora_loaded"], 16)

        for n, (kind, _, cols, rows, src, _) in enumerate(pieces):
            for m in before.get(n, ()):
                i, (l, q) = mod_no[m], m
                if i >= 2:
                    sp.wait_ge(S["wmod_used"], i - 1)
                sp.dma_start(wmod[:, i % 2], A[f"wmod{l}"][:, :, q * D:(q + 1) * D]).then_inc(wmod_in[i % 2], 16)
            if n >= SLOTS:
                sp.wait_ge(S["stage_lo"], n - SLOTS + 1)
                if n - SLOTS in bias_no:
                    sp.wait_ge(S["bias_mm"], bias_no[n - SLOTS])
            dst = stage[0:rows, n % SLOTS, 0:cols]
            if kind == "mask":
                dst = dst.bitcast(I32)
            if len(src.shape) == 3:
                dst = dst.rearrange("p (k n) -> p k n", k=src.shape[1])
            sp.dma_start(dst, src).then_inc(stage_in[n % SLOTS], 16)
            if n == 0:
                load_lora(0)
            if n == 1:
                sp.dma_start(W["ident"][:], A["ident"]).then_inc(W["const_loaded"], 16)
                sp.dma_start(W["ga_bias"][:], A["bias"].to_broadcast([P, D])).then_inc(S["bias_loaded"], 16)
            if n == 3:
                load_lora(1)
            if n == 6:
                load_lora(2)

    @block.tensor
    def _(pe):
        def lora(n):
            kind, no, cols, rows, _, _ = pieces[n]
            r = ("gate", "up", "down").index(kind)
            pe.wait_ge(S["lora_split"], 2 * (r + 1))
            pe.wait_ge(S["lora_hi"], 2 * (r + 1))
            if lora_no[n] > 1:
                pe.wait_ge(S["stage_pre"], pre_no[n] - 1)
            if kind == "down":
                for k in range(no, no + cols // D):
                    mm = pe.matmul(ps_lora[0:hid_rows(k), (k - no) * D:(k - no + 1) * D],
                                   lora_s[:, r % 2, 0, k * P:k * P + hid_rows(k)], lora_s[:, r % 2, 1, 0:D], start=True, stop=True)
            else:
                for a in range(0, HID, D):
                    b = min(HID, a + D)
                    mm = pe.matmul(ps_lora[:, a:b], lora_s[:, r % 2, 0, no * P:(no + 1) * P], lora_s[:, r % 2, 1, a:b],
                                   start=True, stop=True)
            mm.then_inc(S["lora_mm"], 1)

        def meet_shift(n):
            kind, no, _, _, _, _ = pieces[n]
            st = stage[:, n % SLOTS]
            if n in pre_no:
                pe.wait_ge(S["stage_pre"], pre_no[n])
            else:
                pe.wait_ge(stage_in[n % SLOTS], 16 * (n // SLOTS + 1))
            if kind == "win":
                if no == 0:
                    pe.wait_ge(S["mod_done"], mod_no[(1, 0)] + 1)
                    pe.wait_ge(S["stage_pre"], max(pre_no[k] for k in loras))
                for a in range(0, 2 * DI, D):
                    mm = pe.matmul(ps_lora[:, a:a + D], shift_b[:, 0, no, :], st[:, a:a + D], start=(no == 0),
                                   stop=(no == KD - 1))
            else:
                w = RA if kind == "ra" else D
                pe.wait_ge(S["mod_done"], mod_no[(1, 3)] + 1)
                if kind == "ra":
                    pe.wait_ge(S["row_step"], 1)
                for k in range(KD):
                    mm = pe.matmul(ps_row[:, 0:w], shift_b[:, 1, k, :], st[:, k * w:(k + 1) * w],
                                   start=(k == 0), stop=(k == KD - 1))
            mm.then_inc(S["bias_mm"], 1)

        pe.wait_ge(S["silu_cb_done"], 1)
        pe.wait_ge(S["blk_loaded"], 16)
        for n in range(N):
            for m in before.get(n, ()):
                i, (l, q) = mod_no[m], m
                pe.wait_ge(wmod_in[i % 2], 16 * (i // 2 + 1))
                if i >= 2:
                    pe.wait_ge(S["mod_done"], i - 1)
                for k in range(KD):
                    mm = pe.matmul(ps_mod[:, i % 2], silu_cb[:, l, k, :], wmod[:, i % 2, k], start=(k == 0),
                                   stop=(k == KD - 1))
                mm.then_inc(S["wmod_used"], 1)
            if kinds[n] == "mask":
                pe.wait_ge(S["mask_sums"], 1)
                pe.matmul(ps_mask[:, 0:KD * NB], blk32[:], msum[:], start=True, stop=True).then_inc(S["mask_mm"], 1)
            if n in lora_no:
                lora(n)
            if n in bias_no:
                meet_shift(n)

    @block.gpsimd
    def _(pool):
        nc.gpsimd.memset(lora_f[:], 0.0).then_inc(S["lora_zero"], 1)

    @block.scalar
    def _(act):
        def split_lora(r):
            act.wait_ge(S["lora_loaded"], 16 * 6 * (r + 1))
            if r == 2:
                act.wait_ge(S["lora_mm"], KD)
            for j, w in enumerate(lora_widths[r]):
                nc.scalar.activation(lora_s[:, r % 2, j, 0:w], lora_f[:, j, 0:w], ACT.Copy, scale=WS).then_inc(S["lora_hi"], 1)

        act.wait_ge(S["cvec_loaded"], 16)
        nc.scalar.activation(silu_c[:], cvec[:], ACT.Silu).then_inc(S["silu_c_done"], 1)
        split_lora(0)
        for n in range(1, N):
            kind, _, _, rows, _, cuts = pieces[n]
            if n == 4:
                split_lora(1)
            if n == 7:
                split_lora(2)
            act.wait_ge(stage_in[n % SLOTS], 16 * (n // SLOTS + 1))
            if n in pre_no:
                act.wait_ge(S["stage_pre"], pre_no[n])
            if kind in BIAS:
                act.wait_ge(S["mod_done"], mod_no[(1, 1 if kind == "win" else 4)] + 1)
            for a, b, high, low, col in cuts:
                src = stage[0:rows, n % SLOTS, a:b]
                if col is None:
                    op = nc.scalar.activation(high, src, ACT.Copy, scale=WS)
                else:
                    op = nc.scalar.activation(high, src, ACT.Identity, scale=col)
            op.then_inc(S["stage_hi"], 1)

    @block.vector
    def _(dve):
        nc.vector.memset(W["mhalf"][:], -0.5).then_inc(W["mhalf_set"], 1)
        nc.vector.memset(W["ones"][:], 1.0).then_inc(W["mhalf_set"], 1)
        nc.vector.memset(W["epsilon"][:], LN_EPS).then_inc(W["mhalf_set"], 1)
        dve.wait_ge(S["silu_c_done"], 1)
        for l in range(2):
            last = nc.vector.tensor_copy(silu_cb[:, l], silu_c[:, l, :].unsqueeze(2).to_broadcast([P, KD, P]))
        last.then_inc(S["silu_cb_done"], 1)
        step = [0]

        def stepped(op):
            op.then_inc(S["mod_step"], 1)
            step[0] += 1
            dve.wait_ge(S["mod_step"], step[0])

        def diagonal(dst, src, tiles):
            stepped(nc.vector.tensor_tensor(picked[:, 0:tiles], src.rearrange("p (m q) -> p m q", q=P),
                                            W["ident"][:].unsqueeze(1).to_broadcast([P, tiles, P]), ALU.mult))
            return nc.vector.tensor_reduce(dst, picked[:, 0:tiles], X, ALU.add)

        def adaln(m):
            i, (l, q) = mod_no[m], m
            if i:
                dve.wait_ge(S["mod_done"], i)
            dve.wait_ge(S["wmod_used"], i + 1)
            src = ps_mod[:, i % 2]
            if q in (2, 5):
                dst = W["mod0"][:, q // 3, :] if l == 0 else gate1[:, q // 3, :]
                stepped(nc.vector.tensor_scalar(sgn[:], src, 0.0, 2.0, ALU.is_ge, ALU.mult))
                stepped(nc.vector.tensor_copy(dst, src))
                stepped(nc.vector.scalar_tensor_tensor(dst, dst, -1.0, dst, ALU.mult, ALU.max))
                stepped(nc.vector.tensor_scalar(dst, dst, 0.25, 1.0 / WS if l == 0 else 1.0, ALU.max, ALU.mult))
                nc.vector.scalar_tensor_tensor(dst, sgn[:], 1.0, dst, ALU.subtract, ALU.mult).then_inc(S["mod_done"], 1)
                return
            ln = q // 3
            dst = (W["shift0"], W["scale0"], shift, scale)[2 * l + q % 3][:, ln]
            if q % 3 == 0:
                op = diagonal(dst, src, KD)
                if l:
                    stepped(op)
                    op = nc.vector.tensor_copy(shift_b[:, ln], dst.unsqueeze(2).to_broadcast([P, KD, P]))
            else:
                stepped(diagonal(dst, src, KD))
                op = nc.vector.tensor_scalar(dst, dst, 1.0, WS if l else 1.0, ALU.add, ALU.mult)
            op.then_inc(S["mod_done"], 1)
            dve.wait_ge(S["mod_done"], i + 1)

        def biases(n):
            kind = kinds[n]
            if n == last_win:
                dve.wait_ge(S["bias_mm"], bias_no[n])
                dve.wait_ge(S["mod_done"], len(mods))
                for m in range(0, 2 * KI, KD):
                    op = diagonal(W["b_in"][:, m:m + KD], ps_lora[:, m * P:(m + KD) * P], KD)
                    if m + KD < 2 * KI:
                        stepped(op)
                op.then_inc(W["bias_done"], 1)
            if kind in ("base", "ra"):
                dve.wait_ge(S["bias_mm"], bias_no[n])
                w = RA if kind == "ra" else D
                row_h, row_l = (W["rb_h"], W["rb_l"]) if kind == "ra" else (W["bb_h"], W["bb_l"])
                stepped(nc.vector.tensor_scalar(row_h[:], ps_row[0:1, 0:w], WS, None, ALU.mult))
                nc.vector.scalar_tensor_tensor(row_l[:], ps_row[0:1, 0:w], WS, row_h[:], ALU.mult, ALU.subtract)\
                  .then_inc(S["row_step"], 1)

        def split_lora(r):
            dve.wait_ge(S["lora_hi"], 2 * (r + 1))
            for j, (at, w) in enumerate(zip((64, 32), lora_widths[r])):
                low = lora_s[at:at + LORA, r % 2, j, 0:w]
                nc.vector.scalar_tensor_tensor(low, lora_f[at:at + LORA, j, 0:w], WS, low, ALU.mult, ALU.subtract)\
                  .then_inc(S["lora_split"], 1)

        def low_part(n):
            _, _, _, rows, _, cuts = pieces[n]
            dve.wait_ge(S["stage_hi"], n)
            for a, b, high, low, col in cuts:
                op = nc.vector.scalar_tensor_tensor(low, stage[0:rows, n % SLOTS, a:b], WS if col is None else col, high,
                                                    ALU.mult, ALU.subtract)
            op.then_inc(S["stage_lo"], 1)
            biases(n)

        for n in range(N):
            for m in before.get(n, ()):
                if m == (0, 0):
                    dve.wait_ge(W["const_loaded"], 16)
                adaln(m)
                if m == (0, 2):
                    dve.wait_ge(S["mod_done"], mod_no[m] + 1)
                    dve.wait_ge(S["bias_loaded"], 16)
                    nc.vector.scalar_tensor_tensor(W["ga_bias"][:], W["mod0"][:, 0, :], WS, W["ga_bias"][:], ALU.mult, ALU.mult)\
                      .then_inc(W["bias_done"], 1)
            if n in (2, 5, 8):
                split_lora({2: 0, 5: 1, 8: 2}[n])
            kind, no, cols, rows, _, cuts = pieces[n]
            dve.wait_ge(stage_in[n % SLOTS], 16 * (n // SLOTS + 1))
            st = stage[0:rows, n % SLOTS, 0:cols]
            if kind == "mask":
                nc.vector.tensor_reduce(msum[:], st.bitcast(I32).rearrange("p (b w) -> p b w", w=32), X, ALU.add)\
                  .then_inc(S["mask_sums"], 1)
                dve.wait_ge(S["mask_mm"], 1)
                nc.vector.tensor_scalar(mon[:], ps_mask[:, 0:KD * NB], 0.0, None, ALU.is_gt).then_inc(S["stage_lo"], 1)
                dve.wait_ge(S["stage_lo"], 1)
                continue
            if kind == "w0":
                blocks = st.rearrange("p (b w) -> p b w", w=32)
                nc.vector.tensor_tensor(blocks, blocks, mon[:].unsqueeze(2).to_broadcast([P, KD * NB, 32]), ALU.mult)\
                  .then_inc(S["stage_pre"], 1)
            elif kind in ("gate", "up", "down"):
                dve.wait_ge(S["lora_mm"], lora_no[n])
                nc.vector.scalar_tensor_tensor(st, ps_lora[0:rows, 0:cols], 1.0 / (WS * WS), st, ALU.mult, ALU.add)\
                  .then_inc(S["stage_pre"], 1)
            elif kind in ("wout", "base", "lb"):
                q = 2 if kind == "wout" else 5
                dve.wait_ge(S["mod_done"], mod_no[(1, q)] + 1)
                g = gate1[:, q // 3, :]
                if kind == "lb":
                    nc.vector.tensor_tensor(st, st, g, ALU.mult).then_inc(S["stage_pre"], 1)
                else:
                    v = st.rearrange("p (k n) -> p k n", n=D)
                    nc.vector.tensor_tensor(v, v, g.unsqueeze(1).to_broadcast([P, 4, D]), ALU.mult).then_inc(S["stage_pre"], 1)
            if n >= 2:
                low_part(n - 1)
        low_part(N - 1)
        dve.wait_ge(S["stage_lo"], N)
        dve.wait_ge(S["row_step"], 2)
        dve.wait_ge(W["bias_done"], 2)


def products(pe, out, left, right, first=True, last=True):
    n = len(left)
    for k, ((lh, ll), (rh, rl)) in enumerate(zip(left, right)):
        pe.matmul(out, lh, rh, start=(first and k == 0), stop=False)
        pe.matmul(out, lh, rl, start=False, stop=False)
        mm = pe.matmul(out, ll, rh, start=False, stop=(last and k == n - 1))
    return mm


def layer_0(nc, A, x2_dram, W, c, sb, ps, sems):
    xa = sb("xa", [P, TT, D], F32, c)
    xb = sb("xb", [P, TT, D], F32, c)
    x1 = sb("x1", [P, TT, D], F32, c)
    x1r = sb("x1r", [P, TT, D], F32, c)
    scaled = sb("scaled", [P, D], F32, c)
    h1_h = sb("h1_h", [P, KD, CH], F16, c)
    h1_l = sb("h1_l", [P, KD, CH], F16, c)
    h2_h = sb("h2_h", [P, KD, CH], F16, c)
    h2_l = sb("h2_l", [P, KD, CH], F16, c)
    hid_h = sb("hid_h", [P, KH, CH], F16, c)
    hid_l = sb("hid_l", [P, KH, CH], F16, c)
    RING = 3
    sil = sb("sil", [P, RING, CH], F32, c)
    hT = sb("hT", [P, TT, KD, P], F32, c)
    hid = sb("hid", [P, RING, CH], F32, c)
    stats = sb("stats", [P, TT, 6], F32, c)
    mv = sb("mv", [P, TT, 2], F32, c)
    veps = sb("veps", [P, TT], F32, c)
    rstd = sb("rstd", [P, TT], F32, c)
    ps_t = ps("ps_t", [P, TT, KD, P], c)
    ps_gu = ps("ps_gu", [P, 4, 2, CH], c)
    ps_o = ps("ps_o", [P, TT, D], c)
    S = sems("x_loaded xb_done stats_done aggr_done veps_done rstd_done norm_done hT_done t_mm t_hi t_lo "
             "lin_mm o_used x1_done x1r_done gu_mm sil_done hid_done hid_hi hid_lo down_mm x2_done x2_stored met_dve met_pool", c)
    GU_LAG, HID_LAG = 3, 2
    x_v = A["x"].rearrange("(c t p) d -> c p t d", p=P, t=TT)
    x2_v = x2_dram.rearrange("(c t p) d -> c p t d", p=P, t=TT)
    ga, gb = W["mod0"][:, 0, :], W["mod0"][:, 1, :]
    T1_AFTER, LIN_AFTER = 4, 7
    block = c.enter_context(nc.Block())


    @block.sync
    def _(sp):
        sp.dma_start(xa[:], x_v[0]).then_inc(S["x_loaded"], 16)

        def chunk(k):
            sp.wait_ge(S["t_mm"], value(k, 4, 3))
            sp.dma_start(xa[:], x_v[k + 1]).then_inc(S["x_loaded"], 16)

        def store(k):
            sp.wait_ge(S["x2_done"], value(k, TT, 1))
            sp.dma_start(x2_v[k], x1r[:]).then_inc(S["x2_stored"], 16)

        with sp.Fori(0, NCH - 1) as k:
            chunk(k)
            store(k)
        store(NCH - 1)
        sp.wait_ge(S["x2_stored"], 16 * NCH)

    @block.tensor
    def _(pe):
        pe.wait_ge(W["const_loaded"], 16)

        def turn(e):
            for t in range(TT):
                pe.wait_ge(S["norm_done"], e * TT + (t + 1))
                pe.wait_ge(S["t_lo"], e * TT + (t + 1))
                for k in range(KD):
                    tr = pe.transpose(ps_t[:, t, k], xa[:, t, k * P:(k + 1) * P], W["ident"][:])
                tr.then_inc(S["t_mm"], 1)

        def linear(n, first):
            for t in range(TT):
                pe.wait_ge(S["t_lo"], n * (2 * TT) + (TT + TT))
                if not first:
                    pe.wait_ge(S["o_used"], n * (2 * TT) + (t - 3))
                tok = slice(t * P, (t + 1) * P)
                products(pe, ps_o[:, t], [(h1_h[:, k, tok], h1_l[:, k, tok]) for k in range(KD)],
                         [(W["w0_h"][:, k], W["w0_l"][:, k]) for k in range(KD)]).then_inc(S["lin_mm"], 1)

        def gate_up(k, m):
            rows = hid_rows(m)
            cols = slice(m * P, m * P + rows)
            if m == 0:
                pe.wait_ge(S["t_lo"], k * (2 * TT) + (TT + 2 * TT))
            pe.wait_ge(S["hid_done"], k * KH + (m + 1))
            dst = ps_gu[0:rows, m % 4]
            right = [(h2_h[:, i], h2_l[:, i]) for i in range(KD)]
            products(pe, dst[:, 0], [(W["g_h"][:, i, cols], W["g_l"][:, i, cols]) for i in range(KD)], right)
            products(pe, dst[:, 1], [(W["u_h"][:, i, cols], W["u_l"][:, i, cols]) for i in range(KD)], right)\
                .then_inc(S["gu_mm"], 1)

        def down(k, t, last):
            early = KH - 3
            pe.wait_ge(S["hid_lo"], k * KH + (early + HID_LAG))
            pe.wait_ge(S["o_used"], k * (2 * TT) + ((1 if last else 3) + t))
            tok = slice(t * P, (t + 1) * P)
            left = [(hid_h[0:hid_rows(m), m, tok], hid_l[0:hid_rows(m), m, tok]) for m in range(KH)]
            right = [(W["d_h"][0:hid_rows(m), m], W["d_l"][0:hid_rows(m), m]) for m in range(KH)]
            products(pe, ps_o[:, t], left[:early], right[:early], True, False)
            for m in range(early, KH):
                pe.wait_ge(S["hid_lo"], k * KH + (m + 1 + HID_LAG))
                mm = products(pe, ps_o[:, t], left[m:m + 1], right[m:m + 1], False, m == KH - 1)
            mm.then_inc(S["down_mm"], 1)

        turn(0)
        linear(0, True)
        turn(1)
        with pe.Fori(0, NCH - 1) as k:
            for m in range(KH):
                gate_up(k, m)
                if m == T1_AFTER:
                    turn(k * 2 + 2)
                if m == LIN_AFTER:
                    linear(k + 1, False)
            down(k, 0, False)
            turn(k * 2 + 3)
            down(k, 1, False)
        for m in range(KH):
            gate_up(NCH - 1, m)
        for t in range(TT):
            down(NCH - 1, t, True)

    @block.scalar
    def _(act):
        def high(e, ln, dst):
            for t in range(TT):
                act.wait_ge(S["t_mm"], e * TT + (t + 1))
                act.wait_ge(S["t_lo"], e * TT + (t + 1))
                for k in range(KD):
                    op = nc.scalar.activation(hT[:, t, k], ps_t[:, t, k], ACT.Identity, scale=W["scale0"][:, ln, k:k + 1],
                                              bias=W["shift0"][:, ln, k:k + 1])
                op.then_inc(S["hT_done"], 1)
            for t in range(TT):
                act.wait_ge(S["hT_done"], e * TT + (t + 1))
                nc.scalar.activation(dst[:, :, t * P:(t + 1) * P], hT[:, t], ACT.Copy).then_inc(S["t_hi"], 1)

        def silu(k, m):
            rows = hid_rows(m)
            act.wait_ge(S["gu_mm"], value(k, KH, m))
            act.wait_ge(S["hid_done"], k * KH + (m + GU_LAG - HID_LAG + 1))
            nc.scalar.activation(sil[0:rows, m % RING], ps_gu[0:rows, m % 4, 0], ACT.Silu, scale=1.0 / WS)\
              .then_inc(S["sil_done"], 1)

        def hidden_high(k, m):
            rows = hid_rows(m)
            act.wait_ge(S["hid_done"], k * KH + (m + GU_LAG + 1))
            if m == 0:
                act.wait_ge(S["down_mm"], k * TT + TT)
            nc.scalar.activation(hid_h[0:rows, m], hid[0:rows, m % RING], ACT.Copy).then_inc(S["hid_hi"], 1)

        def gate_ups(k, last):
            for m in range(KH):
                silu(k, m)
                if m:
                    hidden_high(k, m - 1)
                if m == T1_AFTER and not last:
                    high(k * 2 + 2, 0, h1_h)
            hidden_high(k, KH - 1)

        high(0, 0, h1_h)
        high(1, 1, h2_h)
        with act.Fori(0, NCH - 1) as k:
            gate_ups(k, False)
            high(k * 2 + 3, 1, h2_h)
        gate_ups(NCH - 1, True)

    @block.gpsimd
    def _(pool):
        pool.wait_ge(W["mhalf_set"], 3)
        pool.sem_inc(S["hid_lo"], HID_LAG)

        def add_bias(n, first):
            pool.wait_ge(S["x_loaded"], n * 16 + 16)
            if not first:
                pool.wait_ge(S["x1_done"], n * TT)
            nc.gpsimd.tensor_tensor(xb[:], xa[:], W["ga_bias"][:].unsqueeze(1).to_broadcast([P, TT, D]), ALU.add)\
              .then_inc(S["xb_done"], 1)

        def inv_std(e):
            pool.wait_ge(S["aggr_done"], e * TT + TT)
            nc.gpsimd.tensor_tensor(veps[:], mv[:, :, 1], W["epsilon"][:], ALU.add).then_inc(S["veps_done"], 1)
            pool.wait_ge(S["veps_done"], e + 1)
            nc.gpsimd.tensor_tensor(rstd[:], veps[:], W["mhalf"][:, 0:TT], ALU.pow).then_inc(S["rstd_done"], 1)

        def hidden_low(k, m):
            rows = hid_rows(m)
            pool.wait_ge(S["hid_hi"], value(k, KH, m))
            nc.gpsimd.tensor_tensor(hid_l[0:rows, m], hid[0:rows, m % RING], hid_h[0:rows, m], ALU.subtract)\
              .then_inc(S["hid_lo"], 1)

        def keep_x1(n, first):
            pool.wait_ge(S["x1_done"], n * TT + TT)
            if not first:
                pool.wait_ge(S["x2_stored"], n * 16)
            pool.sem_inc(S["met_pool"], 1)
            nc.gpsimd.tensor_copy(x1r[:], x1[:]).then_inc(S["x1r_done"], 1)

        add_bias(0, True)
        inv_std(0)
        inv_std(1)
        keep_x1(0, True)
        with pool.Fori(0, NCH - 1) as k:
            for m in range(KH):
                hidden_low(k, m)
                if m == 0:
                    add_bias(k + 1, False)
                    inv_std(k * 2 + 2)
                if m == LIN_AFTER:
                    inv_std(k * 2 + 3)
            keep_x1(k + 1, False)
        for m in range(KH):
            hidden_low(NCH - 1, m)

    @block.vector
    def _(dve):
        dve.sem_inc(S["t_lo"], TT)
        dve.sem_inc(S["hid_done"], GU_LAG)
        dve.sem_inc(S["down_mm"], TT)

        def statistics(e, src):
            for t in range(TT):
                nc.vector.bn_stats(stats[:, t], src[:, t]).then_inc(S["stats_done"], 1)
            for t in range(TT):
                dve.wait_ge(S["stats_done"], e * TT + (t + 1))
                dve.sem_inc(S["met_dve"], 1)
                nc.vector.bn_aggr(mv[:, t], stats[:, t]).then_inc(S["aggr_done"], 1)

        def normalise(e, src):
            dve.wait_ge(S["rstd_done"], e + 1)
            for t in range(TT):
                nc.vector.tensor_scalar(xa[:, t], src[:, t], mv[:, t, 0:1], rstd[:, t:t + 1], ALU.subtract, ALU.mult)\
                  .then_inc(S["norm_done"], 1)

        def low(e, hi, lo):
            for t in range(TT):
                tok = slice(t * P, (t + 1) * P)
                dve.wait_ge(S["t_hi"], e * TT + (t + 1))
                nc.vector.tensor_tensor(lo[:, :, tok], hT[:, t], hi[:, :, tok], ALU.subtract).then_inc(S["t_lo"], 1)

        def hidden(k, m):
            rows = hid_rows(m)
            dve.wait_ge(S["sil_done"], value(k, KH, m))
            dve.wait_ge(S["hid_lo"], k * KH + (m + 1))
            nc.vector.scalar_tensor_tensor(hid[0:rows, m % RING], ps_gu[0:rows, m % 4, 1], 1.0 / WS,
                                           sil[0:rows, m % RING], ALU.mult, ALU.mult).then_inc(S["hid_done"], 1)

        def add_linear(n, first):
            for t in range(TT):
                dve.wait_ge(S["lin_mm"], n * TT + (t + 1))
                nc.vector.tensor_tensor(scaled[:], ps_o[:, t], ga, ALU.mult).then_inc(S["o_used"], 1)
                if first:
                    dve.wait_ge(S["o_used"], t + 1)
                else:
                    dve.wait_ge(S["o_used"], n * (2 * TT) + (t + 1 - TT))
                    dve.wait_ge(S["x1r_done"], n)
                dve.wait_ge(S["xb_done"], n + 1)
                nc.vector.tensor_tensor(x1[:, t], scaled[:], xb[:, t], ALU.add).then_inc(S["x1_done"], 1)
                dve.wait_ge(S["x1_done"], n * TT + (t + 1))

        def add_swiglu(k, t, last):
            dve.wait_ge(S["down_mm"], k * TT + (t + 1 + TT))
            nc.vector.tensor_tensor(scaled[:], ps_o[:, t], gb, ALU.mult).then_inc(S["o_used"], 1)
            dve.wait_ge(S["o_used"], k * (2 * TT) + ((3 if last else 5) + t))
            dve.wait_ge(S["x1r_done"], k + 1)
            nc.vector.tensor_tensor(x1r[:, t], scaled[:], x1r[:, t], ALU.add).then_inc(S["x2_done"], 1)
            dve.wait_ge(S["x2_done"], value(k, TT, t))

        dve.wait_ge(S["x_loaded"], 16)
        statistics(0, xa)
        dve.wait_ge(S["xb_done"], 1)
        normalise(0, xa)
        low(0, h1_h, h1_l)
        add_linear(0, True)
        statistics(1, x1)
        normalise(1, x1)
        low(1, h2_h, h2_l)
        with dve.Fori(0, NCH - 1) as k:
            for m in range(KH):
                hidden(k, m)
                if m == 0:
                    dve.wait_ge(S["x_loaded"], (k + 1) * 16 + 16)
                    statistics(k * 2 + 2, xa)
                if m == 1:
                    dve.wait_ge(S["xb_done"], k + 2)
                    normalise(k * 2 + 2, xa)
                if m == T1_AFTER:
                    low(k * 2 + 2, h1_h, h1_l)
                if m == LIN_AFTER:
                    add_linear(k + 1, False)
                    statistics(k * 2 + 3, x1)
                if m == LIN_AFTER + 1:
                    normalise(k * 2 + 3, x1)
            add_swiglu(k, 0, False)
            low(k * 2 + 3, h2_h, h2_l)
            add_swiglu(k, 1, False)
        for m in range(KH):
            hidden(NCH - 1, m)
        for t in range(TT):
            add_swiglu(NCH - 1, t, True)


def layer_1(nc, A, x2_dram, bt_dram, out, W, c, sb, ps, sems):
    xa = sb("xn", [P, TT, D], F32, c)
    x3 = sb("x3", [P, TT, D], F32, c)
    zb = sb("zb", [P, 2, CH], F32, c)
    b_gh = sb("b_gh", [P, KI], F32, c)
    h3_h = sb("h3_h", [P, KD, CH], F16, c)
    h3_l = sb("h3_l", [P, KD, CH], F16, c)
    taps_raw = sb("taps_raw", [P, KI, TAPS + 1], F32, c)
    taps = sb("taps", [P, KI, TAPS + 1], F32, c)
    d_vec = sb("d_vec", [P, KI], F32, c)
    diag_t = sb("diag_t", [P, KI // 2, TAPS, P], F32, c)
    b_dt = sb("b_dt", [P, KI], F32, c)
    w_dt = sb("w_dt", [RDT, DI], F32, c)
    a_log = sb("a_log", [P, KI, NS], F32, c)
    a_neg = sb("a_neg", [P, KI, NS], F32, c)
    expert = sb("expert", [P, NE], F32, c)
    hist = sb("hist", [P, KI, TAPS - 1], F32, c)
    xw = sb("xw", [P, 2, TAPS - 1 + CH], F32, c)
    cv = sb("cv", [P, 2, CH], F32, c)
    th = sb("th", [P, 2, CH], F32, c)
    u = sb("u", [P, KI, CH], F32, c)
    u_h = sb("uu_h", [P, KI, CH], F16, c)
    u_l = sb("uu_l", [P, KI, CH], F16, c)
    h4_h = u_h[:, 0:KD]
    h4_l = u_h[:, KD:2 * KD]
    ssm = sb("ssm", [P, TT, RDT + 2 * NS], F32, c)
    ssn = sb("ssn", [P, TT, RDT + 2 * NS], F32, c)
    c_cur = sb("c_cur", [P, TT, NS], F32, c)
    msq = sb("msq", [P, TT, 3], F32, c)
    mse = sb("mse", [P, TT, 3], F32, c)
    rms = sb("rms", [P, TT, 3], F32, c)
    tsb = sb("tsb", [RDT + NS, CH], F32, c)
    b_all = sb("b_all", [P, NS, CH], F32, c)
    ab = sb("ab", [P, DG, CH], F32, c)
    dt = sb("dt", [P, KI, CH], F32, c)
    dtu = sb("dtu", [P, KI, CH], F32, c)
    sg = sb("sg", [P, KI, CH], F32, c)
    da = sb("da", [P, AHEAD, DG, 1 + CH], F32, c)
    dbu = sb("dbu", [P, AHEAD, DG, 1 + CH], F32, c)
    h = sb("h", [P, 2, DG, 1 + CH], F32, c)
    carry = sb("carry", [P, STEPS, DG], F32, c)
    acc = sb("acc", [P, TT, DI], F32, c)
    y32 = sb("y32", [P, 2, CH], F32, c)
    y_h = sb("y_h", [P, KI, CH], F16, c)
    y_l = sb("y_l", [P, KI, CH], F16, c)
    stats = sb("stats1", [P, TT, 6], F32, c)
    mv = sb("mv1", [P, TT, 2], F32, c)
    veps = sb("veps1", [P, TT], F32, c)
    rstd = sb("rstd1", [P, TT], F32, c)
    rl = sb("rl", [P, TT, RA], F32, c)
    top = sb("top", [P, TT, 8], F32, c)
    top_at = sb("top_at", [P, TT, 8], U32, c)
    at = sb("at", [P, TT, 2], F32, c)
    gap = sb("gap", [P, TT], F32, c)
    e2 = sb("e2", [P, TT], F32, c)
    e2p = sb("e2p", [P, TT], F32, c)
    inv = sb("inv", [P, TT], F32, c)
    w12 = sb("w12", [P, TT, 2], F32, c)
    wd = sb("wd", [P, 2, TT, NE], F32, c)
    mid = y32[:, 0].rearrange("p (t w) -> p t w", w=ER)
    mid_h = sb("mid_h", [P, TT, P], F16, c)
    mid_l = sb("mid_l", [P, TT, P], F16, c)
    ps_h = ps("ps_h", [P, 2, TT, D], c)
    ps_m = ps("ps_m", [P, 2, D], c)
    ps_s = ps("ps_s", [P, D], c)
    ps_o = ps("ps_o1", [P, D], c)
    S = sems("w1_loaded taps_done diag_done aexp_done aneg_done zeros_done bgh_done "
             "xa_loaded x3_loaded stats_a aggr_a veps_a rstd_a norm_a "
             "stats_b aggr_b veps_b rstd_b norm_b "
             "t3_mm t3_hi t3_lo gate_mm gate_th gate_sg x_mm xw_done conv_pe conv_dve conv_step tanh_done u_done u_hi u_lo wx_mm "
             "ssm_done sq_done ms_done me_done rms_done ssn_done tsb_mm tsb_done bt_stored b_0 b_1 b_2 b_3 "
             "du_done dt_mm dt_abs dt_exp dt_ln dt_done dtu_done c_done "
             "exp_done dbu_done scan_done carry_done hT_done hT_used "
             "y_mm y_done y_hi y_lo wo_mm x3_done t4_mm t4_hi t4_lo ra_mm rl_done "
             "top_done top_at_done at_done gap_done e2_done e2p_done inv_done w1_done w2_done m1_done wd_done "
             "mid_done mid_mm mid_hi mid_lo base_mm out_done out_stored met_dve met_pe met_pool", c)
    b_in = (S["b_0"], S["b_1"], S["b_2"], S["b_3"])
    BQ = NS // 4
    LASTC = NCH - 1
    x2_v = x2_dram.rearrange("(c t p) d -> c p t d", p=P, t=TT)
    out_v = out.rearrange("a (c t p) d -> c p (a t) d", p=P, t=TT)

    USES = STEPS + NDG

    def use_of_step(s):
        return s + 1 + (s >= UB_AT)

    def use_of_init(g):
        return g * (UB_AT + 1)

    def scans_before(i, s):
        return i * STEPS + (s - AHEAD + 1)

    block = c.enter_context(nc.Block())

    @block.sync
    def _(sp):
        sp.dma_start(taps_raw[:], A["conv"]).then_inc(S["w1_loaded"], 16)
        sp.dma_start(d_vec[:], A["D"]).then_inc(S["w1_loaded"], 16)
        sp.dma_start(b_dt[:], A["b_dt"]).then_inc(S["w1_loaded"], 16)
        sp.dma_start(w_dt[:], A["W_dt"]).then_inc(S["w1_loaded"], 16)
        sp.dma_start(a_log[:], A["A_log"]).then_inc(S["w1_loaded"], 16)
        sp.dma_start(expert[:], A["expert"]).then_inc(S["w1_loaded"], 16)

        def load_xa(n):
            sp.dma_start(xa[:], x2_v[n]).then_inc(S["xa_loaded"], 16)

        def spread_b(n, first):
            sp.wait_ge(S["tsb_done"], n + 1)
            sp.dma_start(bt_dram[n].rearrange("a (s t) -> (a s) t", s=NS), tsb[RDT:RDT + NS, :]).then_inc(S["bt_stored"], 16)
            sp.wait_ge(S["bt_stored"], n * 16 + 16)
            for q in range(4):
                if not first:
                    sp.wait_ge(S["dbu_done"], (n - 1) * STEPS + (NS + BQ * q + BQ))
                sp.dma_start(b_all[:, BQ * q:BQ * q + BQ, :],
                             bt_dram[n][:, BQ * q * CH:(BQ * q + BQ) * CH].to_broadcast([P, BQ * CH])
                             .rearrange("p (s t) -> p s t", s=BQ)).then_inc(b_in[q], 16)

        def iteration(i, p, n, first, second):
            if n is not None:
                if first or second:
                    sp.wait_ge(S["t3_mm"], n * TT)
                else:
                    sp.wait_ge(S["t4_mm"], p * TT)
                load_xa(n)
            if p is not None:
                if not second:
                    sp.wait_ge(S["out_stored"], p * 16)
                sp.dma_start(x3[:], x2_v[p]).then_inc(S["x3_loaded"], 16)
            if n is not None:
                spread_b(n, False)
            if p is not None:
                store(p)

        def store(p):
            sp.wait_ge(S["out_done"], value(p, TT, 1))
            sp.dma_start(out_v[p], x3[:]).then_inc(S["out_stored"], 16)

        load_xa(0)
        spread_b(0, True)
        iteration(0, None, 1, True, False)
        iteration(1, 0, 2, False, True)
        with sp.Fori(2, LASTC) as i:
            iteration(i, i - 1, i + 1, False, False)
        iteration(LASTC, LASTC - 1, None, False, False)
        sp.wait_ge(S["out_stored"], LASTC * 16)
        sp.dma_start(x3[:], x2_v[LASTC]).then_inc(S["x3_loaded"], 16)
        store(LASTC)
        sp.wait_ge(S["out_stored"], NCH * 16)

    def at_slot(table, s, lag=1):
        return table.get(s - lag, ())

    @block.tensor
    def _(pe):
        last_s = [None]

        def take_s(sem, val):
            if last_s[0] is not None:
                pe.wait_ge(*last_s[0])
            last_s[0] = (sem, val)

        def turn_in(n, t, dst, t_mm, norm):
            pe.wait_ge(norm, n * TT + (t + 1))
            for k in range(KD):
                tr = pe.transpose(dst[:, k * P:(k + 1) * P], xa[:, t, k * P:(k + 1) * P], W["ident"][:])
            tr.then_inc(t_mm, 1)

        def turn_in_a(n, t):
            take_s(S["t3_lo"], n * TT + (t + 1))
            turn_in(n, t, ps_s, S["t3_mm"], S["norm_a"])

        def turn_in_b(p, t):
            pe.wait_ge(*((S["t4_lo"], p * TT + 1) if t else (S["x3_done"], p * TT + TT)))
            turn_in(p, t, ps_o, S["t4_mm"], S["norm_b"])

        h3 = [(h3_h[:, k], h3_l[:, k]) for k in range(KD)]

        def x_tile(n, m, first):
            if m < 2:
                if not first:
                    pe.wait_ge(S["gate_th"], (n - 1) * KI + (KI - 1 + m))
            else:
                pe.wait_ge(S["xw_done"], n * (3 * KI) + 3 * (m - 1))
            if m == 0:
                pe.wait_ge(S["t3_lo"], n * TT + TT)
            cols = slice(m * P, (m + 1) * P)
            products(pe, ps_m[:, m % 2, 0:CH], [(W["wi_h"][:, k, cols], W["wi_l"][:, k, cols]) for k in range(KD)], h3)\
                .then_inc(S["x_mm"], 1)

        def gate_tile(n, m):
            if m == 0:
                pe.wait_ge(S["ssm_done"], n + 1)
            elif m == 1:
                pe.wait_ge(S["xw_done"], n * (3 * KI) + 3 * KI)
            elif m < 4:
                pe.wait_ge(S["dt_abs"], value(n, KI, m))
            elif m < 6:
                pe.wait_ge(S["dt_abs"], value(n, KI, m + 2))
            else:
                pe.wait_ge(S["gate_th"], n * KI + (m - 1))
            cols = slice(DI + m * P, DI + (m + 1) * P)
            products(pe, ps_m[:, m % 2, 0:CH], [(W["wi_h"][:, k, cols], W["wi_l"][:, k, cols]) for k in range(KD)], h3)\
                .then_inc(S["gate_mm"], 1)

        def dt_tile(n, m):
            if m in (0, 1):
                pe.wait_ge(S["gate_th"], value(n, KI, m))
            elif m in (4, 5):
                pe.wait_ge(S["gate_th"], value(n, KI, m - 2))
            else:
                pe.wait_ge(S["dt_abs"], n * KI + (m - 1))
            if m == 0:
                pe.wait_ge(S["tsb_done"], n + 1)
            pe.matmul(ps_m[:, m % 2, 0:CH], w_dt[:, m * P:(m + 1) * P], tsb[0:RDT, :], start=True, stop=True)\
                .then_inc(S["dt_mm"], 1)

        def wx(n):
            pe.wait_ge(S["xw_done"], n * (3 * KI) + 3 * (KI - 1))
            pe.wait_ge(S["u_lo"], n * KI + KI)
            for t in range(TT):
                tok = slice(t * P, (t + 1) * P)
                mm = products(pe, ps_m[:, 0, t * 64:(t + 1) * 64], [(u_h[:, k, tok], u_l[:, k, tok]) for k in range(KI)],
                              [(W["wx_h"][:, k], W["wx_l"][:, k]) for k in range(KI)])
            mm.then_inc(S["wx_mm"], 1)

        def turn_tsb(n):
            take_s(S["tsb_done"], n + 1)
            pe.wait_ge(S["ssn_done"], n * 2 + 2)
            pe.sem_inc(S["met_pe"], 1)
            for t in range(TT):
                tr = pe.transpose(ps_s[0:RDT + NS, t * P:(t + 1) * P], ssn[:, t, 0:RDT + NS], W["ident"][:])
            tr.then_inc(S["tsb_mm"], 1)

        def convolve(n, m):
            if m % 2:
                return
            take_s(S["tanh_done"], value(n, KI, m))
            pe.wait_ge(S["xw_done"], n * (3 * KI) + (3 * m + 2))
            for tap in range(TAPS):
                mm = pe.matmul(ps_s[:, 0:CH], diag_t[:, m // 2, tap], xw[:, m % 2, tap:tap + CH], start=(tap == 0),
                               stop=(tap == TAPS - 1))
            mm.then_inc(S["conv_pe"], 1)

        def h_bank(i, use, first):
            if not (first and use < 2):
                pe.wait_ge(S["hT_used"], i * USES + (use - 1))
            return use % 2

        def init_acc(i, g, first):
            b = h_bank(i, use_of_init(g), first)
            pe.wait_ge(S["du_done"], i * NDG + (g + 1))
            for t in range(TT):
                for j in range(DG):
                    tr = pe.transpose(ps_h[:, b, t, j * P:(j + 1) * P], ab[:, j, t * P:(t + 1) * P], W["ident"][:])
            tr.then_inc(S["hT_done"], 1)

        def turn_h(i, s, first):
            b = h_bank(i, use_of_step(s), first)
            pe.wait_ge(S["scan_done"], value(i, STEPS, s))
            for t in range(TT):
                for j in range(DG):
                    tr = pe.transpose(ps_h[:, b, t, j * P:(j + 1) * P], h[:, s % 2, j, 1 + t * P:1 + (t + 1) * P], W["ident"][:])
            tr.then_inc(S["hT_done"], 1)

        def turn_y(i, m):
            take_s(S["y_done"], value(i, KI, m))
            if m % DG == 0:
                pe.wait_ge(S["hT_used"], i * USES + (use_of_step(NS - 1 if m == 0 else STEPS - 1) + 1))
            for t in range(TT):
                tr = pe.transpose(ps_s[:, t * P:(t + 1) * P], acc[:, t, m * P:(m + 1) * P], W["ident"][:])
            tr.then_inc(S["y_mm"], 1)

        def out_projection(p, q, first):
            t, part = q // 4, q % 4
            if t == 0:
                pe.wait_ge(S["y_lo"], p * KI + 2 * (part + 1))
            if q == 0:
                if not first:
                    pe.wait_ge(S["out_done"], p * TT)
            if q == 4:
                pe.wait_ge(S["x3_done"], p * TT + 1)
            tok = slice(t * P, (t + 1) * P)
            ks = range(2 * part, 2 * part + 2)
            mm = products(pe, ps_o[:], [(y_h[:, k, tok], y_l[:, k, tok]) for k in ks],
                          [(W["wo_h"][:, k], W["wo_l"][:, k]) for k in ks], part == 0, part == 3)
            if part == 3:
                mm.then_inc(S["wo_mm"], 1)

        def router(p):
            for t in range(TT):
                tok = slice(t * P, (t + 1) * P)
                products(pe, ps_o[:, t * RA:(t + 1) * RA], [(h4_h[:, k, tok], h4_l[:, k, tok]) for k in range(KD)],
                         [(W["ra_h"][:, k], W["ra_l"][:, k]) for k in range(KD)], True, False)
                pe.matmul(ps_o[:, t * RA:(t + 1) * RA], W["ones"][:], W["rb_h"][:], start=False, stop=False)
                mm = pe.matmul(ps_o[:, t * RA:(t + 1) * RA], W["ones"][:], W["rb_l"][:], start=False, stop=True)
            mm.then_inc(S["ra_mm"], 1)

        def turn_mid(p):
            take_s(S["mid_lo"], p + 1)
            pe.wait_ge(S["mid_done"], p + 1)
            for t in range(TT):
                tr = pe.transpose(ps_s[:, t * P:(t + 1) * P], mid[:, t, :], W["ident"][:])
            tr.then_inc(S["mid_mm"], 1)

        def experts(p, q):
            t, part = q // 2, q % 2
            tok = slice(t * P, (t + 1) * P)
            left = [(h4_h[:, k, tok], h4_l[:, k, tok]) for k in range(KD)] + [(mid_h[:, t], mid_l[:, t])]
            right = [(W["ba_h"][:, k], W["ba_l"][:, k]) for k in range(KD)] + [(W["lb_h"][:], W["lb_l"][:])]
            if part == 0:
                if t == 0:
                    pe.wait_ge(S["rl_done"], p + 1)
                else:
                    pe.wait_ge(S["out_done"], p * TT + 1)
                products(pe, ps_o[:], left[:2], right[:2], True, False)
                return
            pe.wait_ge(S["mid_lo"], p + 1)
            products(pe, ps_o[:], left[2:], right[2:], False, False)
            pe.matmul(ps_o[:], W["ones"][:], W["bb_h"][:], start=False, stop=False)
            pe.matmul(ps_o[:], W["ones"][:], W["bb_l"][:], start=False, stop=True).then_inc(S["base_mm"], 1)

        def iteration(i, p, n, first, second):
            for s in range(STEPS):
                if s == 0:
                    init_acc(i, 0, first)
                if s == UB_AT:
                    init_acc(i, 1, first)
                turn_h(i, s, first)
                for m in DTB_AT.get(s, ()):
                    dt_tile(i, m)
                if p is not None:
                    for m in YB_AT.get(s, ()):
                        turn_y(p, m)
                for m in GB_AT.get(s, ()):
                    gate_tile(i, m)
                if n is not None:
                    for t in T3_AT.get(s, ()):
                        turn_in_a(n, t)
                    for m in at_slot(XT_AT, s):
                        convolve(n, m)
                    for m in XT_AT.get(s, ()):
                        x_tile(n, m, False)
                if p is not None:
                    for q in WO_AT.get(s, ()):
                        out_projection(p, q, second)
                for m in YA_AT.get(s, ()):
                    turn_y(i, m)
                if n is not None and s == WX_AT:
                    wx(n)
                if p is not None:
                    for t in T4_AT.get(s, ()):
                        turn_in_b(p, t)
                if n is not None and s == TSB_AT:
                    turn_tsb(n)
                if n is not None and s < TSB_AT:
                    for m in GA_AT.get(s, ()):
                        gate_tile(n, m)
                if p is not None and s == RA_AT:
                    pe.wait_ge(S["t4_lo"], p * TT + TT)
                    router(p)
                if n is not None:
                    for m in DTA_AT.get(s, ()):
                        dt_tile(n, m)
                    if s > TSB_AT:
                        for m in GA_AT.get(s, ()):
                            gate_tile(n, m)
                if p is not None and s == MID_AT:
                    turn_mid(p)
                if p is not None:
                    for q in BASE_AT.get(s, ()):
                        experts(p, q)

        pe.wait_ge(S["diag_done"], KI // 2 * TAPS)
        pe.wait_ge(S["w1_loaded"], 16 * 6)
        for t in range(TT):
            turn_in_a(0, t)
        for m in range(KI):
            x_tile(0, m, True)
            if m:
                convolve(0, m - 1)
        convolve(0, KI - 1)
        wx(0)
        turn_tsb(0)
        gate_tile(0, 0)
        gate_tile(0, 1)
        for m in range(DG):
            dt_tile(0, m)
        gate_tile(0, 2)
        gate_tile(0, 3)
        iteration(0, None, 1, True, False)
        iteration(1, 0, 2, False, True)
        with pe.Fori(2, LASTC) as i:
            last_s[0] = (S["mid_lo"], i - 1)
            iteration(i, i - 1, i + 1, False, False)
        last_s[0] = (S["mid_lo"], LASTC - 1)
        iteration(LASTC, LASTC - 1, None, False, False)
        for m in range(DG, KI):
            turn_y(LASTC, m)
        for q in range(4 * TT):
            out_projection(LASTC, q, False)
        for t in range(TT):
            turn_in_b(LASTC, t)
        pe.wait_ge(S["t4_lo"], NCH * TT)
        router(LASTC)
        turn_mid(LASTC)
        for q in range(2 * TT):
            experts(LASTC, q)


    @block.scalar
    def _(act):
        def exps(i, s, first):
            g, st = s // NS, s % NS
            if not (first and s < AHEAD):
                act.wait_ge(S["scan_done"], scans_before(i, s))
            if not first:
                act.wait_ge(S["carry_done"], (i - 1) * STEPS + (s + 1))
            nc.scalar.activation(dbu[:, s % AHEAD, :, 0], carry[:, s, :], ACT.Copy)
            if st == 0:
                act.wait_ge(S["dt_done"], i * 2 + (g + 1))
            for j in range(DG):
                m = g * DG + j
                ex = nc.scalar.activation(da[:, s % AHEAD, j, 1:], dt[:, m], ACT.Exp, scale=a_neg[:, m, st:st + 1])
            ex.then_inc(S["exp_done"], 1)

        def high(n, t, mm, hi, dst, src):
            act.wait_ge(mm, n * TT + (t + 1))
            nc.scalar.activation(dst[:, :, t * P:(t + 1) * P], src[:].rearrange("p (k q) -> p k q", k=KD), ACT.Copy)\
              .then_inc(hi, 1)

        def x_in(n, m, first):
            act.wait_ge(S["x_mm"], value(n, KI, m))
            if not (first and m < 2):
                act.wait_ge(S["conv_dve"] if m % 2 else S["conv_pe"], n * (KI // 2) + (m // 2))
            nc.scalar.activation(xw[:, m % 2, 0:TAPS - 1], hist[:, m], ACT.Copy).then_inc(S["xw_done"], 1)
            bias = W["b_in"][:, m:m + 1]
            nc.scalar.activation(xw[:, m % 2, TAPS - 1:], ps_m[:, m % 2, 0:CH], ACT.Identity, scale=1.0 / WS, bias=bias)\
              .then_inc(S["xw_done"], 1)
            act.wait_ge(S["xw_done"], n * (3 * KI) + (3 * m + 1))
            nc.scalar.activation(hist[:, m], ps_m[:, m % 2, CH - TAPS + 1:CH], ACT.Identity, scale=1.0 / WS, bias=bias)\
              .then_inc(S["xw_done"], 1)

        def x_tanh(n, m, first):
            act.wait_ge(S["conv_dve"] if m % 2 else S["conv_pe"], n * (KI // 2) + (m // 2 + 1))
            if not (first and m < 2):
                act.wait_ge(S["u_done"], n * KI + (m - 1))
            if not first and m < 2:
                act.wait_ge(S["gate_sg"], n * KI + (m - 1))
            bias = taps[:, m, TAPS:TAPS + 1]
            if m % 2:
                nc.scalar.activation(th[:, m % 2], cv[:, m % 2], ACT.Tanh).then_inc(S["tanh_done"], 1)
                return
            nc.scalar.activation(cv[:, m % 2], ps_s[:, 0:CH], ACT.Identity, bias=bias)
            nc.scalar.activation(th[:, m % 2], ps_s[:, 0:CH], ACT.Tanh, bias=bias).then_inc(S["tanh_done"], 1)

        def u_high(n, m):
            act.wait_ge(S["u_done"], value(n, KI, m))
            nc.scalar.activation(u_h[:, m], u[:, m], ACT.Copy).then_inc(S["u_hi"], 1)

        def gate_tanh(i, m, first=False):
            act.wait_ge(S["gate_mm"], value(i, KI, m))
            if m < 2:
                act.wait_ge(S["u_done"], i * KI + (KI - 1 + m))
            if not (first and m < 2):
                act.wait_ge(S["gate_sg"], i * KI + (m - 1))
            nc.scalar.activation(th[:, m % 2], ps_m[:, m % 2, 0:CH], ACT.Tanh, scale=0.5 / WS, bias=b_gh[:, m:m + 1])
            nc.scalar.activation(zb[:, m % 2], ps_m[:, m % 2, 0:CH], ACT.Identity, scale=1.0 / WS,
                                 bias=W["b_in"][:, KI + m:KI + m + 1]).then_inc(S["gate_th"], 1)

        def dt_abs(n, m, first=False):
            act.wait_ge(S["dt_mm"], value(n, KI, m))
            if m == DG:
                act.wait_ge(S["hT_done"], n * USES + 1)
            if m == 0 and not first:
                act.wait_ge(S["hT_done"], (n - 1) * USES + (use_of_init(1) + 1))
            nc.scalar.activation(dt[:, m], ps_m[:, m % 2, 0:CH], ACT.Identity, bias=b_dt[:, m:m + 1])
            nc.scalar.activation(ab[:, m % DG], ps_m[:, m % 2, 0:CH], ACT.Abs, bias=b_dt[:, m:m + 1]).then_inc(S["dt_abs"], 1)

        def dt_log(n, g):
            act.wait_ge(S["dt_abs"], n * KI + (g + 1) * DG)
            nc.scalar.activation(ab[:], ab[:], ACT.Exp, scale=-1.0).then_inc(S["dt_exp"], 1)
            act.wait_ge(S["dt_exp"], n * 2 + (g + 1))
            nc.scalar.activation(ab[:], ab[:], ACT.Ln, bias=1.0).then_inc(S["dt_ln"], 1)

        def d_u(n, g):
            act.wait_ge(S["dt_done"], n * 2 + (g + 1))
            if g == 0:
                act.wait_ge(S["u_done"], n * KI + KI)
            for j in range(DG):
                m = g * DG + j
                op = nc.scalar.activation(ab[:, j], u[:, m], ACT.Copy, scale=d_vec[:, m:m + 1])
            op.then_inc(S["du_done"], 1)

        def ssm_in(n):
            act.wait_ge(S["wx_mm"], n + 1)
            nc.scalar.activation(ssm[:].rearrange("p t w -> p (t w)"), ps_m[:, 0, 0:TT * 64], ACT.Copy, scale=1.0 / WS)\
              .then_inc(S["ssm_done"], 1)

        def tsb_in(n):
            act.wait_ge(S["tsb_mm"], n + 1)
            nc.scalar.activation(tsb[:], ps_s[0:RDT + NS, 0:CH], ACT.Copy).then_inc(S["tsb_done"], 1)

        def y_high(i, m):
            act.wait_ge(S["y_done"], value(i, KI, m))
            nc.scalar.activation(y_h[:, m], y32[:, m % 2], ACT.Copy).then_inc(S["y_hi"], 1)

        def router_in(p):
            act.wait_ge(S["ra_mm"], p + 1)
            nc.scalar.activation(rl[:].rearrange("p t w -> p (t w)"), ps_o[:, 0:TT * RA], ACT.Copy, scale=1.0 / WS)\
              .then_inc(S["rl_done"], 1)

        def router_exp(p):
            act.wait_ge(S["gap_done"], p + 1)
            nc.scalar.activation(e2[:], gap[:], ACT.Exp).then_inc(S["e2_done"], 1)

        def mid_high(p):
            act.wait_ge(S["mid_mm"], p + 1)
            nc.scalar.activation(mid_h[:].rearrange("p t w -> p (t w)"), ps_s[:, 0:TT * P], ACT.Copy).then_inc(S["mid_hi"], 1)

        def others(i, p, n, first, s):
            for m in at_slot(DTB_AT, s, 2):
                dt_abs(i, m)
            if s == 4:
                dt_log(i, 1)
            if s == 6:
                d_u(i, 1)
            if n is not None and s == 31:
                d_u(n, 0)
            if p is not None:
                for m in at_slot(YB_AT, s, 3):
                    y_high(p, m)
            for m in at_slot(GB_AT, s, 2):
                gate_tanh(i, m)
            if n is not None:
                for t in at_slot(T3_AT, s, 2):
                    high(n, t, S["t3_mm"], S["t3_hi"], h3_h, ps_s)
                for m in at_slot(XT_AT, s, 2):
                    x_in(n, m, False)
                for m in at_slot(XT_AT, s, 4):
                    x_tanh(n, m, False)
                for m in at_slot(XT_AT, s, 6):
                    u_high(n, m)
            for m in at_slot(YA_AT, s, 3):
                y_high(i, m)
            if n is not None and s == WX_AT + 2:
                ssm_in(n)
            if p is not None:
                for t in at_slot(T4_AT, s, 2):
                    high(p, t, S["t4_mm"], S["t4_hi"], h4_h, ps_o)
            if n is not None and s == TSB_AT + 2:
                tsb_in(n)
            if p is not None and s == RA_AT + 2:
                router_in(p)
            if n is not None:
                for m in at_slot(GA_AT, s, 2):
                    gate_tanh(n, m)
                for m in at_slot(DTA_AT, s, 2):
                    dt_abs(n, m)
                if s == 29:
                    dt_log(n, 0)
            if p is not None and s == RA_AT + 3:
                router_exp(p)
            if p is not None and s == MID_AT + 2:
                mid_high(p)

        def iteration(i, p, n, first):
            for s in range(STEPS):
                exps(i, s, first)
                if s:
                    others(i, p, n, first, s - 1)
            others(i, p, n, first, STEPS - 1)

        act.wait_ge(S["w1_loaded"], 16 * 6)
        nc.scalar.activation(a_neg[:], a_log[:], ACT.Exp).then_inc(S["aexp_done"], 1)
        act.wait_ge(S["aneg_done"], 1)
        act.wait_ge(S["bgh_done"], 1)
        act.wait_ge(S["zeros_done"], 3)
        for t in range(TT):
            high(0, t, S["t3_mm"], S["t3_hi"], h3_h, ps_s)
        for m in range(KI + 2):
            if m < KI:
                x_in(0, m, True)
            if 1 <= m < KI + 1:
                x_tanh(0, m - 1, True)
            if m >= 2:
                u_high(0, m - 2)
        ssm_in(0)
        tsb_in(0)
        gate_tanh(0, 0, True)
        gate_tanh(0, 1, True)
        for m in range(DG):
            dt_abs(0, m, True)
        gate_tanh(0, 2)
        gate_tanh(0, 3)
        dt_log(0, 0)
        d_u(0, 0)
        iteration(0, None, 1, True)
        iteration(1, 0, 2, False)
        with act.Fori(2, LASTC) as i:
            iteration(i, i - 1, i + 1, False)
        iteration(LASTC, LASTC - 1, None, False)
        for m in range(DG, KI):
            y_high(LASTC, m)
        for t in range(TT):
            high(LASTC, t, S["t4_mm"], S["t4_hi"], h4_h, ps_o)
        router_in(LASTC)
        router_exp(LASTC)
        mid_high(LASTC)

    @block.gpsimd
    def _(pool):
        def db(i, s, first):
            g, st = s // NS, s % NS
            if st % BQ == 0 and g == 0:
                pool.wait_ge(b_in[st // BQ], i * 16 + 16)
            if st == 0:
                pool.wait_ge(S["dtu_done"], i * 2 + (g + 1))
            if not (first and s < AHEAD):
                pool.wait_ge(S["scan_done"], scans_before(i, s))
            nc.gpsimd.tensor_tensor(dbu[:, s % AHEAD, :, 1:], dtu[:, g * DG:(g + 1) * DG],
                                    b_all[:, st, :].unsqueeze(1).to_broadcast([P, DG, CH]), ALU.mult).then_inc(S["dbu_done"], 1)

        def inv_std(n, aggr, ve, rs):
            pool.wait_ge(aggr, n * TT + TT)
            nc.gpsimd.tensor_tensor(veps[:], mv[:, :, 1], W["epsilon"][:], ALU.add).then_inc(ve, 1)
            pool.wait_ge(ve, n + 1)
            nc.gpsimd.tensor_tensor(rstd[:], veps[:], W["mhalf"][:, 0:TT], ALU.pow).then_inc(rs, 1)

        def u_low(n, m):
            pool.wait_ge(S["u_hi"], value(n, KI, m))
            nc.gpsimd.tensor_tensor(u_l[:, m], u[:, m], u_h[:, m], ALU.subtract).then_inc(S["u_lo"], 1)

        def y_low(i, m):
            pool.wait_ge(S["y_hi"], value(i, KI, m))
            nc.gpsimd.tensor_tensor(y_l[:, m], y32[:, m % 2], y_h[:, m], ALU.subtract).then_inc(S["y_lo"], 1)

        def rms_pow(n):
            pool.wait_ge(S["me_done"], n * 2 + 2)
            nc.gpsimd.tensor_tensor(rms[:].rearrange("p t w -> p (t w)"), mse[:].rearrange("p t w -> p (t w)"),
                                    W["mhalf"][:, 0:TT * 3], ALU.pow).then_inc(S["rms_done"], 1)

        def dt_u(n, g):
            pool.wait_ge(S["dt_done"], n * 2 + (g + 1))
            grp = slice(g * DG, (g + 1) * DG)
            nc.gpsimd.tensor_tensor(dtu[:, grp], dt[:, grp], u[:, grp], ALU.mult).then_inc(S["dtu_done"], 1)

        def others(i, p, n, first, s):
            if p is not None:
                for m in at_slot(YB_AT, s, 4):
                    y_low(p, m)
            if n is not None and s == 3:
                inv_std(n, S["aggr_a"], S["veps_a"], S["rstd_a"])
            if s == 5:
                dt_u(i, 1)
            if n is not None:
                for m in at_slot(XT_AT, s, 7):
                    u_low(n, m)
            for m in at_slot(YA_AT, s, 4):
                y_low(i, m)
            if p is not None and s == 19:
                inv_std(p, S["aggr_b"], S["veps_b"], S["rstd_b"])
            if n is not None and s == 23:
                rms_pow(n)
            if n is not None and s == 30:
                dt_u(n, 0)

        def iteration(i, p, n, first):
            for s in range(STEPS):
                db(i, s, first)
                if s:
                    others(i, p, n, first, s - 1)
            others(i, p, n, first, STEPS - 1)

        inv_std(0, S["aggr_a"], S["veps_a"], S["rstd_a"])
        for m in range(KI):
            u_low(0, m)
        rms_pow(0)
        dt_u(0, 0)
        iteration(0, None, 1, True)
        iteration(1, 0, 2, False)
        with pool.Fori(2, LASTC) as i:
            iteration(i, i - 1, i + 1, False)
        iteration(LASTC, LASTC - 1, None, False)
        for m in range(DG, KI):
            y_low(LASTC, m)
        inv_std(LASTC, S["aggr_b"], S["veps_b"], S["rstd_b"])

    @block.vector
    def _(dve):
        def scans(i, s, first):
            dve.wait_ge(S["exp_done"], value(i, STEPS, s))
            dve.wait_ge(S["dbu_done"], value(i, STEPS, s))
            if not (first and s < 2):
                dve.wait_ge(S["carry_done"], i * STEPS + (s - 1))
            hs, das, dbs = (x.rearrange("p j t -> p (j t)") for x in (h[:, s % 2], da[:, s % AHEAD], dbu[:, s % AHEAD]))
            nc.vector.tensor_tensor_scan(hs, das, dbs, 0.0, ALU.mult, ALU.add)\
              .then_inc(S["scan_done"], 1)

        def add_state(i, s):
            g, st, use = s // NS, s % NS, use_of_step(s)
            dve.wait_ge(S["hT_done"], value(i, USES, use))
            dve.wait_ge(S["hT_used"], i * USES + use)
            for t in range(TT):
                part = acc[:, t, g * DG * P:(g + 1) * DG * P]
                op = nc.vector.scalar_tensor_tensor(part, ps_h[:, use % 2, t], c_cur[:, t, st:st + 1], part,
                                                    ALU.mult, ALU.add)
            op.then_inc(S["hT_used"], 1)

        def keep_state(i, s):
            dve.wait_ge(S["scan_done"], value(i, STEPS, s))
            nc.vector.tensor_copy(carry[:, s, :], h[:, s % 2, :, CH]).then_inc(S["carry_done"], 1)

        def start_acc(i, g, first):
            use = use_of_init(g)
            dve.wait_ge(S["hT_done"], value(i, USES, use))
            if not first:
                dve.wait_ge(S["y_mm"], (i - 1) * KI + (g + 1) * DG)
            for t in range(TT):
                cp = nc.vector.tensor_copy(acc[:, t, g * DG * P:(g + 1) * DG * P], ps_h[:, use % 2, t])
            cp.then_inc(S["hT_used"], 1)

        def keep_c(i, first):
            if not first:
                dve.wait_ge(S["hT_used"], i * USES)
            nc.vector.tensor_copy(c_cur[:], ssn[:, :, RDT + NS:]).then_inc(S["c_done"], 1)
            dve.wait_ge(S["c_done"], i + 1)

        def statistics(n, src, st, ag):
            for t in range(TT):
                nc.vector.bn_stats(stats[:, t], src[:, t]).then_inc(st, 1)
            for t in range(TT):
                dve.wait_ge(st, n * TT + (t + 1))
                dve.sem_inc(S["met_dve"], 1)
                nc.vector.bn_aggr(mv[:, t], stats[:, t]).then_inc(ag, 1)

        def normalise(n, src, rs, norm):
            dve.wait_ge(rs, n + 1)
            for t in range(TT):
                nc.vector.tensor_scalar(xa[:, t], src[:, t], mv[:, t, 0:1], rstd[:, t:t + 1], ALU.subtract, ALU.mult)\
                  .then_inc(norm, 1)

        def low(n, t, hi, lo, src, dst, bank):
            dve.wait_ge(hi, n * TT + (t + 1))
            tok = slice(t * P, (t + 1) * P)
            nc.vector.tensor_tensor(dst[:, :, tok], bank[:].rearrange("p (k q) -> p k q", k=KD), src[:, :, tok],
                                    ALU.subtract).then_inc(lo, 1)

        def convolve(n, m, first):
            if m % 2 == 0:
                return
            dve.wait_ge(S["xw_done"], n * (3 * KI) + (3 * m + 2))
            if not (first and m < 2):
                dve.wait_ge(S["u_done"], n * KI + (m - 1))
            for a, tap in enumerate(range(TAPS - 1, -1, -1)):
                w = taps[:, m, tap:tap + 1]
                src = xw[:, m % 2, tap:tap + CH]
                if a == 0:
                    op = nc.vector.tensor_scalar(cv[:, m % 2], src, w, taps[:, m, TAPS:TAPS + 1], ALU.mult, ALU.add)
                else:
                    dve.wait_ge(S["conv_step"], n * (3 * (KI // 2)) + (3 * (m // 2) + a))
                    op = nc.vector.scalar_tensor_tensor(cv[:, m % 2], src, w, cv[:, m % 2], ALU.mult, ALU.add)
                op.then_inc(S["conv_dve"] if a == TAPS - 1 else S["conv_step"], 1)

        def make_u(n, m):
            dve.wait_ge(S["tanh_done"], value(n, KI, m))
            nc.vector.scalar_tensor_tensor(u[:, m], th[:, m % 2], 1.0, cv[:, m % 2], ALU.add, ALU.mult).then_inc(S["u_done"], 1)

        def make_sg(i, m, first=False):
            dve.wait_ge(S["gate_th"], value(i, KI, m))
            if not first:
                dve.wait_ge(S["y_done"], (i - 1) * KI + (m + 1))
            nc.vector.scalar_tensor_tensor(sg[:, m], th[:, m % 2], 1.0, zb[:, m % 2], ALU.add, ALU.mult).then_inc(S["gate_sg"], 1)

        def dt_add(n, g):
            dve.wait_ge(S["dt_ln"], n * 2 + (g + 1))
            grp = slice(g * DG, (g + 1) * DG)
            nc.vector.scalar_tensor_tensor(dt[:, grp], dt[:, grp], 0.0, ab[:], ALU.max, ALU.add).then_inc(S["dt_done"], 1)

        def mean_squares(n):
            dve.wait_ge(S["ssm_done"], n + 1)
            nc.vector.tensor_tensor(ssn[:], ssm[:], ssm[:], ALU.mult).then_inc(S["sq_done"], 1)
            dve.wait_ge(S["sq_done"], n + 1)
            nc.vector.tensor_reduce(msq[:, :, 0:1], ssn[:, :, 0:RDT].unsqueeze(2), X, ALU.add).then_inc(S["ms_done"], 1)
            nc.vector.tensor_reduce(msq[:, :, 1:3], ssn[:, :, RDT:].rearrange("p t (b s) -> p t b s", b=2), X, ALU.add)\
              .then_inc(S["ms_done"], 1)
            dve.wait_ge(S["ms_done"], n * 2 + 2)
            nc.vector.tensor_scalar(mse[:, :, 0:1], msq[:, :, 0:1], 1.0 / RDT, RMS_EPS, ALU.mult, ALU.add).then_inc(S["me_done"], 1)
            nc.vector.tensor_scalar(mse[:, :, 1:3], msq[:, :, 1:3], 1.0 / NS, RMS_EPS, ALU.mult, ALU.add).then_inc(S["me_done"], 1)

        def rms_apply(n):
            dve.wait_ge(S["rms_done"], n + 1)
            nc.vector.tensor_tensor(ssn[:, :, 0:RDT], ssm[:, :, 0:RDT], rms[:, :, 0:1].to_broadcast([P, TT, RDT]), ALU.mult)\
              .then_inc(S["ssn_done"], 1)
            nc.vector.tensor_tensor(ssn[:, :, RDT:].rearrange("p t (b s) -> p t b s", b=2),
                                    ssm[:, :, RDT:].rearrange("p t (b s) -> p t b s", b=2),
                                    rms[:, :, 1:3].unsqueeze(3).to_broadcast([P, TT, 2, NS]), ALU.mult).then_inc(S["ssn_done"], 1)

        def make_y(i, m, first):
            dve.wait_ge(S["y_mm"], value(i, KI, m))
            if not (first and m < 2):
                dve.wait_ge(S["y_lo"], i * KI + (m - 1))
            nc.vector.scalar_tensor_tensor(y32[:, m % 2], ps_s[:, 0:CH], 0.5, sg[:, m], ALU.mult, ALU.mult)\
              .then_inc(S["y_done"], 1)

        def add_out_projection(p, t):
            dve.wait_ge(S["wo_mm"], value(p, TT, t))
            dve.wait_ge(S["x3_loaded"], p * 16 + 16)
            nc.vector.scalar_tensor_tensor(x3[:, t], ps_o[:], 1.0 / WS, x3[:, t], ALU.mult, ALU.add).then_inc(S["x3_done"], 1)

        def choose(p):
            dve.wait_ge(S["rl_done"], p + 1)
            dve.sem_inc(S["met_dve"], 1)
            for t in range(TT):
                nc.vector.max(top[:, t], rl[:, t, 0:NE]).then_inc(S["top_done"], 1)
            for t in range(TT):
                dve.wait_ge(S["top_done"], p * TT + (t + 1))
                dve.sem_inc(S["met_dve"], 1)
                nc.vector.max_index(top_at[:, t], top[:, t], rl[:, t, 0:NE]).then_inc(S["top_at_done"], 1)
            nc.vector.tensor_tensor(gap[:], top[:, :, 1], top[:, :, 0], ALU.subtract).then_inc(S["gap_done"], 1)
            dve.wait_ge(S["top_at_done"], p * TT + TT)
            nc.vector.tensor_copy(at[:], top_at[:, :, 0:2]).then_inc(S["at_done"], 1)

        def weigh(p):
            dve.wait_ge(S["e2_done"], p + 1)
            nc.vector.tensor_scalar(e2p[:], e2[:], 1.0, None, ALU.add).then_inc(S["e2p_done"], 1)
            dve.wait_ge(S["e2p_done"], p + 1)
            nc.vector.reciprocal(inv[:], e2p[:]).then_inc(S["inv_done"], 1)
            dve.wait_ge(S["inv_done"], p + 1)
            nc.vector.tensor_scalar(w12[:, :, 0], inv[:], 2.0, None, ALU.mult).then_inc(S["w1_done"], 1)
            dve.wait_ge(S["w1_done"], p + 1)
            nc.vector.tensor_tensor(w12[:, :, 1], w12[:, :, 0], e2[:], ALU.mult).then_inc(S["w2_done"], 1)
            dve.wait_ge(S["w2_done"], p + 1)
            dve.wait_ge(S["at_done"], p + 1)
            for t in range(TT):
                for b in range(2):
                    nc.vector.tensor_scalar(wd[:, b, t], expert[:], at[:, t, b:b + 1], w12[:, t, b:b + 1],
                                            ALU.is_equal, ALU.mult).then_inc(S["m1_done"], 1)
            dve.wait_ge(S["m1_done"], p * (2 * TT) + 2 * TT)
            nc.vector.tensor_tensor(wd[:, 0], wd[:, 0], wd[:, 1], ALU.add).then_inc(S["wd_done"], 1)
            dve.wait_ge(S["wd_done"], p + 1)
            nc.vector.tensor_tensor(mid.rearrange("p t (e r) -> p t e r", e=NE),
                                    rl[:, :, NE:].rearrange("p t (e r) -> p t e r", e=NE),
                                    wd[:, 0].unsqueeze(3).to_broadcast([P, TT, NE, LORA]), ALU.mult).then_inc(S["mid_done"], 1)

        def mid_low(p):
            dve.wait_ge(S["mid_hi"], p + 1)
            nc.vector.tensor_tensor(mid_l[:].rearrange("p t w -> p (t w)"), ps_s[:, 0:TT * P],
                                    mid_h[:].rearrange("p t w -> p (t w)"), ALU.subtract).then_inc(S["mid_lo"], 1)

        def add_experts(p, t):
            dve.wait_ge(S["base_mm"], value(p, TT, t))
            nc.vector.scalar_tensor_tensor(x3[:, t], ps_o[:], 1.0 / WS, x3[:, t], ALU.mult, ALU.add).then_inc(S["out_done"], 1)

        def iteration(i, p, n, first, second):
            for s in range(STEPS):
                scans(i, s, first)
                if s == 0 and not first:
                    add_state(i - 1, STEPS - 1)
                if s == 0:
                    keep_c(i, first)
                if s == 1:
                    start_acc(i, 0, first)
                if s == UB_AT + 1:
                    start_acc(i, 1, first)
                if s:
                    add_state(i, s - 1)
                keep_state(i, s)
                if s == 3:
                    dt_add(i, 1)
                if p is not None:
                    for m in at_slot(YB_AT, s):
                        make_y(p, m, False)
                if n is not None and s == 1:
                    dve.wait_ge(S["xa_loaded"], n * 16 + 16)
                    statistics(n, xa, S["stats_a"], S["aggr_a"])
                if n is not None and s == 2:
                    normalise(n, xa, S["rstd_a"], S["norm_a"])
                for m in at_slot(GB_AT, s, 2):
                    make_sg(i, m, first)
                if n is not None:
                    for t in at_slot(T3_AT, s):
                        low(n, t, S["t3_hi"], S["t3_lo"], h3_h, h3_l, ps_s)
                    for m in at_slot(XT_AT, s, 4):
                        make_u(n, m)
                    for m in at_slot(XT_AT, s, 2):
                        convolve(n, m, False)
                if p is not None and s == 8:
                    add_out_projection(p, 0)
                if p is not None and s == 16:
                    add_out_projection(p, 1)
                if p is not None and s == 17:
                    dve.wait_ge(S["x3_done"], p * TT + TT)
                    statistics(p, x3, S["stats_b"], S["aggr_b"])
                if p is not None and s == 18:
                    normalise(p, x3, S["rstd_b"], S["norm_b"])
                for m in at_slot(YA_AT, s):
                    make_y(i, m, first)
                if n is not None:
                    for m in at_slot(GA_AT, s, 2):
                        make_sg(n, m)
                if n is not None and s == WX_AT + 2:
                    mean_squares(n)
                if n is not None and s == WX_AT + 3:
                    rms_apply(n)
                if p is not None:
                    for t in at_slot(T4_AT, s):
                        low(p, t, S["t4_hi"], S["t4_lo"], h4_h, h4_l, ps_o)
                if p is not None and s == RA_AT + 1:
                    choose(p)
                if p is not None and s == RA_AT + 2:
                    weigh(p)
                if n is not None and s == 29:
                    dt_add(n, 0)
                if p is not None and s == MID_AT + 1:
                    mid_low(p)
                if p is not None:
                    for q in at_slot(BASE_AT, s):
                        if q % 2:
                            add_experts(p, q // 2)

        nc.vector.memset(da[:, :, :, 0], 0.0).then_inc(S["zeros_done"], 1)
        nc.vector.memset(hist[:], 0.0).then_inc(S["zeros_done"], 1)
        nc.vector.memset(carry[:], 0.0).then_inc(S["zeros_done"], 1)
        dve.wait_ge(S["w1_loaded"], 16 * 6)
        nc.vector.tensor_scalar(taps[:], taps_raw[:], 0.5, None, ALU.mult).then_inc(S["taps_done"], 1)
        dve.wait_ge(S["taps_done"], 1)
        for m in range(0, KI, 2):
            for tap in range(TAPS):
                nc.vector.tensor_scalar(diag_t[:, m // 2, tap], W["ident"][:], taps[:, m, tap:tap + 1], None, ALU.mult)\
                  .then_inc(S["diag_done"], 1)
        nc.vector.tensor_scalar(b_gh[:], W["b_in"][:, KI:], 0.5, None, ALU.mult).then_inc(S["bgh_done"], 1)
        dve.wait_ge(S["aexp_done"], 1)
        nc.vector.tensor_scalar(a_neg[:], a_neg[:], -1.0, None, ALU.mult).then_inc(S["aneg_done"], 1)
        dve.wait_ge(S["taps_done"], 1)
        dve.wait_ge(S["zeros_done"], 3)
        dve.wait_ge(S["xa_loaded"], 16)
        statistics(0, xa, S["stats_a"], S["aggr_a"])
        normalise(0, xa, S["rstd_a"], S["norm_a"])
        for t in range(TT):
            low(0, t, S["t3_hi"], S["t3_lo"], h3_h, h3_l, ps_s)
        for m in range(KI):
            convolve(0, m, True)
            make_u(0, m)
        mean_squares(0)
        rms_apply(0)
        make_sg(0, 0, True)
        make_sg(0, 1, True)
        dt_add(0, 0)
        make_sg(0, 2, True)
        make_sg(0, 3, True)
        iteration(0, None, 1, True, False)
        iteration(1, 0, 2, False, True)
        with dve.Fori(2, LASTC) as i:
            iteration(i, i - 1, i + 1, False, False)
        iteration(LASTC, LASTC - 1, None, False, False)
        add_state(LASTC, STEPS - 1)
        for m in range(DG, KI):
            make_y(LASTC, m, False)
        for t in range(TT):
            add_out_projection(LASTC, t)
        dve.wait_ge(S["x3_done"], NCH * TT)
        statistics(LASTC, x3, S["stats_b"], S["aggr_b"])
        normalise(LASTC, x3, S["rstd_b"], S["norm_b"])
        for t in range(TT):
            low(LASTC, t, S["t4_hi"], S["t4_lo"], h4_h, h4_l, ps_o)
        choose(LASTC)
        weigh(LASTC)
        mid_low(LASTC)
        for t in range(TT):
            add_experts(LASTC, t)


def kernel(**inputs):
    import numpy as np
    import concourse.bacc as bacc
    from concourse.bass_utils import run_bass_kernel_spmd

    I = {k: np.asarray(v) for k, v in inputs.items()}
    arrays = {
        "x": I["L0_attn_data"].reshape(T, D),
        "mask": I["L0_attn_mask"].T, "w0": I["L0_attn_weight"].T, "bias": I["L0_attn_bias"].reshape(1, D),
        "gate_w": I["L0_ffn_gate_w"].T, "up_w": I["L0_ffn_up_w"].T, "down_w": I["L0_ffn_down_w"].T,
        "gate_a": I["L0_ffn_gate_a"], "gate_b": I["L0_ffn_gate_b"].T,
        "up_a": I["L0_ffn_up_a"], "up_b": I["L0_ffn_up_b"].T,
        "down_a": I["L0_ffn_down_a"], "down_b": I["L0_ffn_down_b"].T,
        "c": np.stack([I["L0_c"].reshape(KD, P), I["L1_c"].reshape(KD, P)]).transpose(2, 0, 1),
        "wmod0": I["L0_wmod"], "wmod1": I["L1_wmod"],
        "W_in": I["L1_attn_W_in"].T,
        "conv": np.concatenate([I["L1_attn_conv_w"], I["L1_attn_conv_b"].reshape(DI, 1)], axis=1)
        .reshape(KI, P, TAPS + 1).transpose(1, 0, 2),
        "W_x": I["L1_attn_W_x"].T, "W_dt": I["L1_attn_W_dt"].T,
        "b_dt": I["L1_attn_b_dt"].reshape(KI, P).T,
        "A_log": I["L1_attn_A_log"].reshape(KI, P, NS).transpose(1, 0, 2),
        "D": I["L1_attn_D"].reshape(KI, P).T,
        "W_out": I["L1_attn_W_out"].T, "base_W": I["L1_ffn_base_W"].T,
        "router_A": np.concatenate([I["L1_ffn_router_W"].T, I["L1_ffn_lora_A"].transpose(1, 0, 2).reshape(D, ER)], axis=1),
        "lora_B": I["L1_ffn_lora_B"].reshape(ER, D),
        "ident": np.eye(P, dtype=np.float32),
        "blk32": np.kron(np.eye(P // 32, dtype=np.float32), np.ones((32, 32), np.float32)),
        "expert": np.tile(np.arange(NE, dtype=np.float32), (P, 1)),
    }
    nc = bacc.Bacc("TRN2", target_bir_lowering=False, num_devices=1, dynamic_dma_scratch_size=1024)
    A, feed = {}, {}
    for name, a in arrays.items():
        a = np.ascontiguousarray(a)
        feed[f"in_{name}"] = a
        A[name] = nc.dram_tensor(f"in_{name}", a.shape, mybir.dt.from_np(a.dtype), kind="ExternalInput").ap()
    for name in ("mask", "w0", "wmod0", "wmod1", "W_out", "base_W", "W_x", "router_A"):
        A[name] = A[name].rearrange("(k p) n -> p k n", p=P)
    for name in ("gate_w", "up_w", "W_in"):
        A[name] = A[name].rearrange("(k p) n -> k p n", p=P)
    out = nc.dram_tensor("out", (1, T, D), F32, kind="ExternalOutput").ap()
    build(nc, A, out)
    r = run_bass_kernel_spmd(nc, [feed], core_ids=[0])
    return r.results[0]["out"]
```
